# Optimizing a Trainium2 kernel written in Bass

```python
import numpy as np
import jax
import jax.numpy as jnp

def _softmax(x, axis=-1):
    return jax.nn.softmax(x, axis=axis)
def _gelu(x):
    return jax.nn.gelu(x, approximate=True)
def _silu(x):
    return jax.nn.silu(x)
def _sigmoid(x):
    return jax.nn.sigmoid(x)
def _layernorm(x, axis=-1, eps=1e-5):
    m = jnp.mean(x, axis=axis, keepdims=True)
    v = jnp.var(x, axis=axis, keepdims=True)
    return (x - m) / jnp.sqrt(v + eps)
def _scatter_add(tgt, idx, src, axis=0):
    return tgt.at[idx].add(src)
def _segment_sum(src, seg, n):
    return jax.ops.segment_sum(src, seg, n)

kernel_name = 'mk_conv_preact_d2_conv_nchw96_4a6551'

def setup_inputs(seed: int = 0):
    np.random.seed(seed)
    _w = jnp.asarray
    def _rec_inputs():
        import jax
        import jax.numpy as jnp
        _gk = jax.random.key(seed)
        x = -4.65e-05 + 0.9999 * jax.random.normal(jax.random.fold_in(_gk, 1), (32, 96, 128, 128), jnp.float32)
        return x
    x = _rec_inputs()
    def _L0_conv_setup():
        import jax, jax.numpy as jnp
        import numpy as np
        DIM = 96
        K = 3
        STRIDE = 1
        PAD = 1
        RED = 4
        BN_EPS = 1e-05

        def _dynamic_weight(x, w1, gamma, beta, running_mean, running_var, w2, b2):
            pooled = jnp.mean(x, axis=(2, 3))
            h1 = pooled @ w1.T
            h1 = (h1 - running_mean) * jax.lax.rsqrt(running_var + BN_EPS) * gamma + beta
            h1 = jax.nn.sigmoid(h1)
            wdyn = h1 @ w2.T + b2
            return wdyn.reshape(x.shape[0], DIM, K, K)

        def _per_sample_depthwise(x, weight, bias):

            def one(xi, wi):
                out = jax.lax.conv_general_dilated(xi[None], wi[:, None], window_strides=(STRIDE, STRIDE), padding=[(PAD, PAD), (PAD, PAD)], dimension_numbers=('NCHW', 'OIHW', 'NCHW'), feature_group_count=DIM)
                return out[0]
            y = jax.vmap(one)(x, weight)
            return y + bias[None, :, None, None]
        key = jax.random.key(seed)
        ks = jax.random.split(key, 8)
        b, c, h, w = (32, DIM, 128, 128)
        cr = DIM // RED
        return {'x': jax.random.normal(ks[0], (b, c, h, w), jnp.float32), 'w1': jax.random.normal(ks[1], (cr, c), jnp.float32) * 0.1, 'gamma': jnp.ones((cr,), jnp.float32), 'beta': jnp.zeros((cr,), jnp.float32), 'running_mean': jax.random.normal(ks[2], (cr,), jnp.float32) * 0.1, 'running_var': jax.random.uniform(ks[3], (cr,), jnp.float32, 0.5, 1.5), 'w2': jax.random.normal(ks[4], (DIM * K * K, cr), jnp.float32) * 0.1, 'b2': jax.random.normal(ks[5], (DIM * K * K,), jnp.float32) * 0.1, 'bias': jnp.zeros((DIM,), jnp.float32)}
    _L0_conv_all = _L0_conv_setup()
    _L0_conv_in = {k: v for k, v in _L0_conv_all.items() if k in ('w1', 'gamma', 'beta', 'running_mean', 'running_var', 'w2', 'b2', 'bias', )}
    del _L0_conv_all

    def _L1_conv_setup():
        import jax, jax.numpy as jnp
        import numpy as np
        import math
        ALPHA = 0.65
        KSIZE = 9

        def _make_y(size):
            ii = jnp.arange(size, dtype=jnp.float32)
            coords = jnp.stack(jnp.meshgrid(ii, ii, indexing='ij'), axis=-1)
            origin = jnp.array([size // 2, size // 2], dtype=jnp.float32)
            return coords - origin

        def _diffusion_kernel(diff_metric, t=1.0):
            y = _make_y(KSIZE)
            z = jnp.einsum('cij,hwj->chwi', diff_metric, y)
            r2 = jnp.sum(z * z, axis=-1)
            alpha = ALPHA
            teff = t ** (1.0 / alpha)
            c1 = 1.0 / math.gamma(1.0 + 1.0 / alpha)
            c2 = math.sqrt(2.0 * c1)
            val = 3.0 * (-2.0 + (1.0 + 2.0 * alpha) * c2) / ((1.0 + 2.0 * alpha) * (-2.0 * c1 + 3.0 * c2))
            tg = c1 * teff
            gauss = 1.0 / (4.0 * math.pi * tg) * jnp.exp(-r2 / (4.0 * tg))
            tp = c2 * math.sqrt(teff)
            poi = math.gamma(1.5) / math.pi ** 1.5 * tp / jnp.power(tp * tp + r2, 1.5)
            return val * gauss + (1.0 - val) * poi
        key = jax.random.key(seed)
        k1, k2 = jax.random.split(key)
        x = jax.random.normal(k1, (16, 96, 224, 224), dtype=jnp.float32)
        bound = math.sqrt(0.5)
        diff_metric = jax.random.uniform(k2, (96, 2, 2), dtype=jnp.float32, minval=-bound, maxval=bound)
        return {'x': x, 'diff_metric': diff_metric}
    _L1_conv_all = _L1_conv_setup()
    _L1_conv_in = {k: v for k, v in _L1_conv_all.items() if k in ('diff_metric', )}
    del _L1_conv_all

    return {
        "x": x,
        "L0_conv_w1": _L0_conv_in["w1"],
        "L0_conv_gamma": _L0_conv_in["gamma"],
        "L0_conv_beta": _L0_conv_in["beta"],
        "L0_conv_running_mean": _L0_conv_in["running_mean"],
        "L0_conv_running_var": _L0_conv_in["running_var"],
        "L0_conv_w2": _L0_conv_in["w2"],
        "L0_conv_b2": _L0_conv_in["b2"],
        "L0_conv_bias": _L0_conv_in["bias"],
        "L1_conv_diff_metric": _L1_conv_in["diff_metric"],
    }

def reference(x, L0_conv_w1, L0_conv_gamma, L0_conv_beta, L0_conv_running_mean, L0_conv_running_var, L0_conv_w2, L0_conv_b2, L0_conv_bias, L1_conv_diff_metric):
    import jax
    import jax.numpy as jnp
    def _L0_conv_ref(x, w1, gamma, beta, running_mean, running_var, w2, b2, bias):
        import jax, jax.numpy as jnp
        import numpy as np
        DIM = 96
        K = 3
        STRIDE = 1
        PAD = 1
        RED = 4
        BN_EPS = 1e-05

        def _dynamic_weight(x, w1, gamma, beta, running_mean, running_var, w2, b2):
            pooled = jnp.mean(x, axis=(2, 3))
            h1 = pooled @ w1.T
            h1 = (h1 - running_mean) * jax.lax.rsqrt(running_var + BN_EPS) * gamma + beta
            h1 = jax.nn.sigmoid(h1)
            wdyn = h1 @ w2.T + b2
            return wdyn.reshape(x.shape[0], DIM, K, K)

        def _per_sample_depthwise(x, weight, bias):

            def one(xi, wi):
                out = jax.lax.conv_general_dilated(xi[None], wi[:, None], window_strides=(STRIDE, STRIDE), padding=[(PAD, PAD), (PAD, PAD)], dimension_numbers=('NCHW', 'OIHW', 'NCHW'), feature_group_count=DIM)
                return out[0]
            y = jax.vmap(one)(x, weight)
            return y + bias[None, :, None, None]
        weight = _dynamic_weight(x, w1, gamma, beta, running_mean, running_var, w2, b2)
        return _per_sample_depthwise(x, weight, bias)

    def _L1_conv_ref(x, diff_metric):
        import jax, jax.numpy as jnp
        import numpy as np
        import math
        ALPHA = 0.65
        KSIZE = 9

        def _make_y(size):
            ii = jnp.arange(size, dtype=jnp.float32)
            coords = jnp.stack(jnp.meshgrid(ii, ii, indexing='ij'), axis=-1)
            origin = jnp.array([size // 2, size // 2], dtype=jnp.float32)
            return coords - origin

        def _diffusion_kernel(diff_metric, t=1.0):
            y = _make_y(KSIZE)
            z = jnp.einsum('cij,hwj->chwi', diff_metric, y)
            r2 = jnp.sum(z * z, axis=-1)
            alpha = ALPHA
            teff = t ** (1.0 / alpha)
            c1 = 1.0 / math.gamma(1.0 + 1.0 / alpha)
            c2 = math.sqrt(2.0 * c1)
            val = 3.0 * (-2.0 + (1.0 + 2.0 * alpha) * c2) / ((1.0 + 2.0 * alpha) * (-2.0 * c1 + 3.0 * c2))
            tg = c1 * teff
            gauss = 1.0 / (4.0 * math.pi * tg) * jnp.exp(-r2 / (4.0 * tg))
            tp = c2 * math.sqrt(teff)
            poi = math.gamma(1.5) / math.pi ** 1.5 * tp / jnp.power(tp * tp + r2, 1.5)
            return val * gauss + (1.0 - val) * poi
        C = x.shape[1]
        kern = _diffusion_kernel(diff_metric, t=1.0)
        rhs = kern[:, None, :, :]
        return jax.lax.conv_general_dilated(x, rhs, window_strides=(1, 1), padding='SAME', dimension_numbers=('NCHW', 'OIHW', 'NCHW'), feature_group_count=C)

    def _gn(v, G=32, eps=1e-5):
        B_, C_, H_, W_ = v.shape
        g = v.reshape(B_, G, C_ // G, H_, W_)
        m = jnp.mean(g, axis=(2, 3, 4), keepdims=True)
        s = jnp.var(g, axis=(2, 3, 4), keepdims=True)
        return ((g - m) / jnp.sqrt(s + eps)).reshape(v.shape)

    def _ln_c(v, eps=1e-6):
        m = jnp.mean(v, axis=1, keepdims=True)
        s = jnp.var(v, axis=1, keepdims=True)
        return (v - m) / jnp.sqrt(s + eps)

    def _ln_t(v, eps=1e-5):
        m = jnp.mean(v, axis=-1, keepdims=True)
        s = jnp.var(v, axis=-1, keepdims=True)
        return (v - m) / jnp.sqrt(s + eps)

    def _to_tokens(v):
        B_, C_, H_, W_ = v.shape
        return v.reshape(B_, C_, H_ * W_).transpose(0, 2, 1)
    def _from_tokens(t, like):
        B_, C_, H_, W_ = like.shape
        return t.transpose(0, 2, 1).reshape(B_, C_, H_, W_)

    x = x + _L0_conv_ref(_gn(x), L0_conv_w1, L0_conv_gamma, L0_conv_beta, L0_conv_running_mean, L0_conv_running_var, L0_conv_w2, L0_conv_b2, L0_conv_bias)
    x = x + _L1_conv_ref(_gn(x), L1_conv_diff_metric)
    return x


_drawn_inputs = setup_inputs


def setup_inputs(seed=0):
    import zlib

    import numpy as np

    out = dict(_drawn_inputs(seed))
    spreads = {'L0_conv_gamma': (1.0, 0.6), 'L0_conv_beta': (0.0, 0.318), 'L0_conv_bias': (0.0, 0.1)}
    factors = {'L0_conv_w1': 200.0, 'L0_conv_running_var': 200.0, 'L0_conv_running_mean': 16.075}
    for name, (base, spread) in spreads.items():
        noise = np.random.default_rng([zlib.crc32(name.encode()), seed]).standard_normal(out[name].shape)
        drawn = base * np.exp(spread * noise) if base else spread * noise
        out[name] = jnp.asarray(drawn.astype(out[name].dtype))
    for name, factor in factors.items():
        out[name] = (out[name] * factor).astype(out[name].dtype)
    return out
```

```python
from contextlib import ExitStack
import math

import concourse.bass as bass
from concourse import mybir

F32 = mybir.dt.float32
F16 = mybir.dt.float16
ALU = mybir.AluOpType
ACT = mybir.ActivationFunctionType

B, C, H, W = 32, 96, 128, 128
G = 32
GC = C // G
IMG = H * W
RED = C // 4
EPS = 1e-5

UB = 4
QN = B // UB
UNITS = G * QN
IMAGES = GC * UB
BANK = UB * W

K0, K1 = 3, 9
P0 = -(-H // K0)
P1 = -(-H // K1)
W0 = P0 * K0
W1 = P1 * K1 + 1

SX = 2.0 ** 8
SW = 2.0 ** 16

ALPHA = 0.65
C1 = 1.0 / math.gamma(1.0 + 1.0 / ALPHA)
C2 = math.sqrt(2.0 * C1)
VAL = 3.0 * (-2.0 + (1.0 + 2.0 * ALPHA) * C2) / ((1.0 + 2.0 * ALPHA) * (-2.0 * C1 + 3.0 * C2))
GAUSS = VAL / (4.0 * math.pi * C1)
POISSON = (1.0 - VAL) * math.gamma(1.5) / math.pi ** 1.5 * C2

CHUNKS = 4
CHUNK = IMG // CHUNKS
BN = 512
STATS = CHUNK // BN

HEAD, TAIL = 2, 4

TC = 24


def statistics_block(nc, ctx, t, d, sem):
    def sb(name, shape, dt=F32):
        return ctx.enter_context(nc.sbuf_tensor(name, shape, dt))

    piece = [sb(f"piece{i}", [C, CHUNK]) for i in range(CHUNKS)]
    bn = sb("bn", [C, B, CHUNKS * STATS, 6])
    mv = sb("mv", [C, B, 2])
    small = {n: sb(n, [C, B]) for n in ("gmean", "dev", "var", "vare", "sd", "rs", "t1", "t2", "pooled", "hlin", "hsig", "hm")}
    col = {n: sb(n, [C, 1]) for n in ("rve", "rsd", "rr", "c1", "c2", "bnscale")}
    group_sum = sb("group_sum", [C, C])
    w1rep = sb("w1rep", [C, C])
    bnvec = sb("bnvec", [C, 7])
    first_of_group = sb("first_of_group", [C, G])
    wide = sb("wide", [C, G, B])
    ones = sb("ones", [C, H])
    biasb = sb("biasb", [H, C])
    dm = sb("dm", [H, C, 4])
    y0 = sb("y0", [H, K1])
    y1 = sb("y1", [H, K1])
    zrow = sb("zrow", [H, TC, K1])
    zcol = sb("zcol", [H, TC, K1])
    za, zb, zc, zd = (sb(n, [H, TC * K1 * K1]) for n in ("za", "zb", "zc", "zd"))

    ps = ctx.enter_context(nc.psum_tensor("ps_small", [H, 512], F32))
    pwide = ctx.enter_context(nc.psum_tensor("ps_wide", [H, 2, 512], F32))

    piece_loaded = [sem(f"piece_loaded{i}") for i in range(CHUNKS)]
    piece_read = sem("piece_read")
    consts_loaded = sem("consts_loaded")
    chain = sem("vector_chain")
    psum_ready = sem("psum_ready")
    to_psum = sem("to_psum")
    to_act = sem("to_act")
    act_done = sem("act_done")
    taps_z = sem("taps_z")

    block = ctx.enter_context(nc.Block())

    @block.sync
    def _(sp):
        for dst, src in ((group_sum, d["group_sum"]), (w1rep, d["w1rep"]), (bnvec, d["bnvec"]),
                         (first_of_group, d["first_of_group"]), (biasb, d["biasb"]), (dm, d["dm"]),
                         (y0, d["y0"]), (y1, d["y1"]), (t["mask0"], d["mask0"]), (t["mask1"], d["mask1"]),
                         (t["classes"], d["classes"]), (t["w2rot"], d["w2rot"])):
            sp.dma_start(dst[:], src).then_inc(consts_loaded, 16)
        for i in range(CHUNKS):
            sp.dma_start(piece[i][:], d["xs"][0, :, i * CHUNK:(i + 1) * CHUNK]).then_inc(piece_loaded[i], 16)
        with sp.Fori(1, B) as b:
            for i in range(CHUNKS):
                sp.wait_ge(piece_read, CHUNKS * (b - 1) + i + 1)
                sp.dma_start(piece[i][:], d["xs"][bass.ds(b, 1), :, i * CHUNK:(i + 1) * CHUNK]
                             .rearrange("a c n -> (a c) n")).then_inc(piece_loaded[i], 16)

    @block.vector
    def _(dve):
        count = [0]

        def link(ins):
            count[0] += 1
            ins.then_inc(chain, 1)
            dve.wait_ge(chain, count[0])

        with dve.Fori(0, B) as b:
            for i in range(CHUNKS):
                dve.wait_ge(piece_loaded[i], 16 * b + 16)
                for j in range(STATS):
                    ins = dve.bn_stats(bn[:, bass.ds(b, 1), i * STATS + j, :].rearrange("c a s -> c (a s)"),
                                       piece[i][:, j * BN:(j + 1) * BN])
                ins.then_inc(piece_read, 1)
        dve.wait_ge(piece_read, B * CHUNKS)
        for b in range(B):
            ins = dve.bn_aggr(mv[:, b, :], bn[:, b, :, :].rearrange("c n s -> c (n s)"))
        link(ins)
        s = small
        dve.tensor_copy(s["t1"][:], mv[:, :, 0]).then_inc(to_psum, 1)
        dve.wait_ge(psum_ready, 1)
        link(dve.tensor_scalar(s["gmean"][:], ps[0:C, 0:B], 1.0 / GC, None, ALU.mult))
        link(dve.tensor_tensor(s["dev"][:], mv[:, :, 0], s["gmean"][:], ALU.subtract))
        link(dve.tensor_tensor(s["t2"][:], s["dev"][:], s["dev"][:], ALU.mult))
        dve.tensor_tensor(s["var"][:], s["t2"][:], mv[:, :, 1], ALU.add).then_inc(to_psum, 1)
        dve.wait_ge(psum_ready, 2)
        dve.tensor_scalar(s["vare"][:], ps[0:C, B:2 * B], 1.0 / GC, EPS, ALU.mult, ALU.add).then_inc(to_act, 1)
        dve.wait_ge(act_done, 1)
        link(dve.reciprocal(s["rs"][:], s["sd"][:]))
        link(dve.tensor_tensor(s["t1"][:], s["rs"][:], s["rs"][:], ALU.mult))
        link(dve.tensor_tensor(s["t2"][:], s["t1"][:], s["vare"][:], ALU.mult))
        link(dve.tensor_scalar(s["t1"][:], s["t2"][:], -0.5, 1.5, ALU.mult, ALU.add))
        link(dve.tensor_tensor(s["hm"][:], s["rs"][:], s["t1"][:], ALU.mult))
        link(dve.tensor_copy(s["rs"][:], s["hm"][:]))
        dve.tensor_tensor(s["pooled"][:], s["dev"][:], s["rs"][:], ALU.mult).then_inc(to_psum, 1)
        dve.wait_ge(consts_loaded, 16 * 12)
        dve.tensor_scalar(col["rve"][:], bnvec[:, 3:4], EPS, None, ALU.add).then_inc(to_act, 1)
        dve.wait_ge(act_done, 2)
        link(dve.reciprocal(col["rr"][:], col["rsd"][:]))
        link(dve.tensor_tensor(col["c1"][:], col["rr"][:], col["rr"][:], ALU.mult))
        link(dve.tensor_tensor(col["c2"][:], col["c1"][:], col["rve"][:], ALU.mult))
        link(dve.tensor_scalar(col["c1"][:], col["c2"][:], -0.5, 1.5, ALU.mult, ALU.add))
        link(dve.tensor_tensor(col["c2"][:], col["rr"][:], col["c1"][:], ALU.mult))
        link(dve.tensor_tensor(col["bnscale"][:], col["c2"][:], bnvec[:, 0:1], ALU.mult))
        dve.wait_ge(psum_ready, 3)
        dve.tensor_scalar(s["hlin"][:], ps[0:C, 2 * B:3 * B], bnvec[:, 2:3], col["bnscale"][:, 0:1],
                          ALU.subtract, ALU.mult).then_inc(to_act, 1)
        dve.wait_ge(act_done, 3)
        link(dve.tensor_scalar(s["hm"][:], s["hsig"][:], bnvec[:, 4:5], bnvec[:, 5:6], ALU.mult, ALU.add))
        fog = first_of_group[:].unsqueeze(2).broadcast_to([C, G, B])
        dve.tensor_tensor(wide[:], fog, s["gmean"][:].unsqueeze(1).broadcast_to([C, G, B]), ALU.mult).then_inc(to_psum, 1)
        dve.wait_ge(psum_ready, 4)
        pw = pwide[:].rearrange("p a n -> p (a n)")
        link(dve.tensor_scalar(t["negmean"][:], pw, -1.0, None, ALU.mult))
        for c in range(GC):
            dve.tensor_tensor(
                t["shift"][:].rearrange("p (g q c b) -> p g q c b", q=QN, c=GC, b=UB)[:, :, :, c, :],
                biasb[:].rearrange("p (g c) -> p g c", c=GC)[:, :, c:c + 1].unsqueeze(3).broadcast_to([H, G, QN, UB]),
                t["negmean"][:].rearrange("p (g q b) -> p g q b", q=QN, b=UB), ALU.subtract)
        dve.tensor_tensor(wide[:], fog, s["rs"][:].unsqueeze(1).broadcast_to([C, G, B]), ALU.mult).then_inc(to_psum, 1)
        dve.wait_ge(psum_ready, 5)
        link(dve.tensor_tensor(t["hidden"][:], pw[0:C, :].rearrange("p (g b) -> p g b", b=B),
                               s["hm"][:].unsqueeze(1).broadcast_to([C, G, B]), ALU.mult))
        hid = t["hidden"][:].rearrange("p g b -> p (g b)")
        link(dve.tensor_scalar(hid, hid, bnvec[:, 6:7], None, ALU.add))

        full = [H, TC, K1, K1]
        for n in range(C // TC):
            dn = dm[:, n * TC:(n + 1) * TC, :]
            for i in range(2):
                link(dve.tensor_tensor(zrow[:], dn[:, :, 2 * i:2 * i + 1].broadcast_to([H, TC, K1]),
                                       y0[:].unsqueeze(1).broadcast_to([H, TC, K1]), ALU.mult))
                link(dve.tensor_tensor(zcol[:], dn[:, :, 2 * i + 1:2 * i + 2].broadcast_to([H, TC, K1]),
                                       y1[:].unsqueeze(1).broadcast_to([H, TC, K1]), ALU.mult))
                z = za if i == 0 else zb
                link(dve.tensor_tensor(z[:].rearrange("p (c x j) -> p c x j", x=K1, j=K1),
                                       zrow[:].unsqueeze(2).broadcast_to(full),
                                       zcol[:].unsqueeze(3).broadcast_to(full), ALU.add))
            link(dve.tensor_tensor(zc[:], za[:], za[:], ALU.mult))
            link(dve.tensor_tensor(za[:], zb[:], zb[:], ALU.mult))
            link(dve.tensor_tensor(zb[:], zc[:], za[:], ALU.add))
            dve.tensor_scalar(zc[:], zb[:], C2 * C2, None, ALU.add).then_inc(taps_z, 1)
            dve.wait_ge(act_done, 5 + 2 * n)
            link(dve.tensor_scalar(zb[:], zb[:], GAUSS * SW, None, ALU.mult))
            link(dve.reciprocal(zd[:], za[:]))
            link(dve.tensor_tensor(zd[:], zd[:], zc[:], ALU.mult))
            link(dve.tensor_tensor(za[:], za[:], zd[:], ALU.add))
            link(dve.tensor_tensor(za[:], za[:], zc[:], ALU.mult))
            link(dve.reciprocal(zd[:], za[:]))
            link(dve.scalar_tensor_tensor(za[:], zd[:], 2.0 * POISSON * SW, zb[:], ALU.mult, ALU.add))
            part = slice(n * TC * K1 * K1, (n + 1) * TC * K1 * K1)
            link(dve.tensor_copy(t["taps_hi"][:, part], za[:]))
            link(dve.tensor_tensor(t["taps_lo"][:, part], za[:], t["taps_hi"][:, part], ALU.subtract))

    @block.scalar
    def _(act):
        act.wait_ge(to_act, 1)
        nc.scalar.activation(small["sd"][:], small["vare"][:], ACT.Sqrt).then_inc(act_done, 1)
        act.wait_ge(to_act, 2)
        nc.scalar.activation(col["rsd"][:], col["rve"][:], ACT.Sqrt).then_inc(act_done, 1)
        act.wait_ge(to_act, 3)
        nc.scalar.activation(small["hsig"][:], small["hlin"][:], ACT.Sigmoid, bias=bnvec[:, 1:2]).then_inc(act_done, 1)
        for n in range(C // TC):
            act.wait_ge(taps_z, n + 1)
            nc.scalar.activation(za[:], zc[:], ACT.Sqrt).then_inc(act_done, 1)
            nc.scalar.activation(zb[:], zb[:], ACT.Exp, scale=-1.0 / (4.0 * C1)).then_inc(act_done, 1)

    @block.gpsimd
    def _(pool):
        nc.gpsimd.memset(ones[:], 1.0).then_inc(t["ones_set"], 1)
        nc.gpsimd.memset(t["average"][:], 0.5 / H).then_inc(t["ones_set"], 1)

    @block.tensor
    def _(pe):
        pe.wait_ge(consts_loaded, 16 * 12)
        pe.wait_ge(t["ones_set"], 2)
        steps = ((group_sum, small["t1"], 0), (group_sum, small["var"], B), (w1rep, small["pooled"], 2 * B))
        for n, (lhs, rhs, at) in enumerate(steps):
            pe.wait_ge(to_psum, n + 1)
            nc.tensor.matmul(ps[0:C, at:at + B], lhs[:], rhs[:], start=True, stop=True).then_inc(psum_ready, 1)
        for n in range(2):
            pe.wait_ge(to_psum, 4 + n)
            for a in range(2):
                ins = nc.tensor.matmul(pwide[:, a, :], ones[:], wide[:].rearrange("c g b -> c (g b)")[:, a * 512:(a + 1) * 512],
                                       start=True, stop=True)
            ins.then_inc(psum_ready, 1)


def main_block(nc, ctx, t, d, sem):
    def sb(name, shape, dt=F32):
        return ctx.enter_context(nc.sbuf_tensor(name, shape, dt))

    xt = [sb(f"xt{i}", [H, GC, UB, W]) for i in range(2)]
    band0 = [sb(f"band0_{i}", [H, IMAGES * K0, W0]) for i in range(2)]
    x1 = [sb(f"x1_{i}", [H, GC, UB, W]) for i in range(2)]
    norm = sb("norm", [H, GC, UB, W])
    hi = [sb(f"hi{i}", [H, GC, UB, W], F16) for i in range(2)]
    lo = [sb(f"lo{i}", [H, GC, UB, W], F16) for i in range(2)]
    y = [sb(f"result{i}", [H, GC, UB, W]) for i in range(2)]
    band1_hi = [sb(f"band1_hi{i}", [H, GC * K1, W1], F16) for i in range(2)]
    band1_lo = [sb(f"band1_lo{i}", [H, GC * K1, W1], F16) for i in range(2)]
    wmix = [sb(f"wmix{i}", [C, IMAGES * K0 * K0]) for i in range(2)]
    bnp = sb("bnp", [H, UB, 6])
    dvp = sb("dvp", [H, UB, 2])
    sqp = sb("sqp", [H, UB, 2])
    vap = sb("vap", [H, UB, 2])
    gm = sb("gm", [H, UB])
    vare = sb("vare1", [H, UB])
    sd = sb("sd1", [H, UB])
    rs0 = sb("rs0", [H, UB])
    n1 = sb("n1", [H, UB])
    n2 = sb("n2", [H, UB])
    n3 = sb("n3", [H, UB])
    rs1 = [sb(f"rs1_{i}", [H, UB]) for i in range(2)]
    nb1 = [sb(f"nb1_{i}", [H, UB]) for i in range(2)]

    def psum(name, shape):
        return ctx.enter_context(nc.psum_tensor(name, shape, F32))

    p0 = [psum(f"p0_{c}", [H, UB, W]) for c in range(GC)]
    p1 = [psum(f"p1_{c}", [H, UB, W]) for c in range(GC)]
    pw = psum("pw", [H, 512])
    pst = psum("pst", [H, 512])

    x_loaded = [sem(f"x_loaded{i}") for i in range(2)]
    centred = sem("centred")
    mixed = sem("mixed")
    taps0_ready = sem("taps0_ready")
    band0_built = sem("band0_built")
    conv0_done = sem("conv0_done")
    evac0_done = sem("evac0_done")
    stats_local = sem("stats_local")
    mean_ready = sem("mean_ready")
    var_local = sem("var_local")
    var_ready = sem("var_ready")
    vare_ready = sem("vare_ready")
    sd_ready = sem("sd_ready")
    scales_ready = sem("scales_ready")
    normalised = sem("normalised")
    split_done = sem("split_done")
    band1_built = sem("band1_built")
    conv1_done = sem("conv1_done")
    evac1_done = sem("evac1_done")
    stored = [sem(f"stored{i}") for i in range(2)]
    mean_chain = sem("mean_chain")
    scale_chain = sem("scale_chain")

    block = ctx.enter_context(nc.Block())

    def pairs(eng, body):
        def samples(g, gslot, start, end):
            with eng.Fori(start // 2, end // 2) as m:
                for k in range(2):
                    body(g, 2 * m + k, QN * g + 2 * m + k, k, gslot)
        for q in range(HEAD):
            body(0, q, q, q % 2, 0)
        samples(0, 0, HEAD, QN)
        samples(1, 1, 0, QN)
        with eng.Fori(1, G // 2 - 1) as n:
            samples(2 * n, 0, 0, QN)
            samples(2 * n + 1, 1, 0, QN)
        samples(G - 2, 0, 0, QN)
        samples(G - 1, 1, 0, QN - TAIL)
        for q in range(QN - TAIL, QN):
            body(G - 1, q, QN * (G - 1) + q, q % 2, 1)

    def known(u):
        return isinstance(u, int)

    @block.sync
    def _(sp):
        def load(g, q, u, slot, gslot):
            if not (known(u) and u < 2):
                sp.wait_ge(conv0_done, GC * (u - 2) + GC)
            for c in range(GC):
                src = d["x_units"][bass.ds(g, 1), bass.ds(q, 1), c, :, :, :]
                sp.dma_start(xt[slot][:, c, :, :], src.rearrange("g q b h w -> h (g q b) w")).then_inc(x_loaded[slot], 16)
        for q in range(2):
            load(0, q, q, q, 0)
        with sp.Fori(1, QN // 2) as m:
            for k in range(2):
                load(0, 2 * m + k, 2 * m + k, k, 0)
        with sp.Fori(1, G) as g:
            with sp.Fori(0, QN // 2) as m:
                for k in range(2):
                    load(g, 2 * m + k, QN * g + 2 * m + k, k, 0)

    @block.scalar
    def _(act):
        def centre(u, slot):
            act.wait_ge(x_loaded[slot], 16 * GC // 2 * (u - slot) + 16 * GC)
            for b in range(UB):
                ins = nc.scalar.activation(xt[slot][:, :, b, :], xt[slot][:, :, b, :], ACT.Identity,
                                           bias=t["negmean"][:, bass.ds(UB * u + b, 1)])
            ins.then_inc(centred, 1)

        def normalise(u, slot):
            act.wait_ge(vare_ready, u + 1)
            nc.scalar.activation(sd[:], vare[:], ACT.Sqrt).then_inc(sd_ready, 1)
            act.wait_ge(scales_ready, u + 1)
            if not (known(u) and u < 1):
                act.wait_ge(split_done, u)
            if not (known(u) and u < 2):
                act.wait_ge(conv1_done, GC * (u - 2) + GC)
            for out in (norm, hi[slot]):
                for b in range(UB):
                    ins = nc.scalar.activation(out[:, :, b, :], x1[slot][:, :, b, :], ACT.Identity,
                                               bias=nb1[slot][:, b:b + 1], scale=rs1[slot][:, b:b + 1])
            ins.then_inc(normalised, 1)

        def store(g, q, u, slot):
            for c in range(GC):
                act.wait_ge(evac1_done, GC * u + c + 1)
                dst = d["out_units"][bass.ds(g, 1), bass.ds(q, 1), c, :, :, :]
                act.dma_start(dst.rearrange("g q b h w -> h (g q b) w"), y[slot][:, c, :, :]).then_inc(stored[slot], 16)

        centre(0, 0)
        centre(1, 1)
        normalise(0, 0)
        centre(2, 0)
        normalise(1, 1)

        def step(g, q, u, slot, gslot):
            if not (known(u) and u + 3 >= UNITS):
                centre(u + 3, 1 - slot)
            store(g, q, u, slot)
            if not (known(u) and u + 2 >= UNITS):
                normalise(u + 2, slot)

        pairs(act, step)
        for slot in range(2):
            act.wait_ge(stored[slot], 16 * GC * UNITS // 2)

    @block.gpsimd
    def _(pool):
        def mix(g, q, u, slot, gslot):
            if not (known(u) and u < 2):
                pool.wait_ge(taps0_ready, u - 1)
            shape = [C, GC, UB, K0 * K0]
            w2g = t["w2rot"][:, bass.ds(g * GC * K0 * K0, GC * K0 * K0)].rearrange("k (c r) -> k c r", c=GC)
            hid = t["hidden"][:].rearrange("k g b -> k (g b)")[:, bass.ds(UB * u, UB)]
            nc.gpsimd.tensor_tensor(wmix[slot][:].rearrange("k (c b r) -> k c b r", c=GC, b=UB),
                                    w2g.unsqueeze(2).broadcast_to(shape),
                                    hid.unsqueeze(1).unsqueeze(3).broadcast_to(shape), ALU.mult).then_inc(mixed, 1)

        def band1(g, gslot):
            if not (known(g) and g < 2):
                pool.wait_ge(conv1_done, GC * QN * (g - 1))
            n = GC * K1
            shape = [H, n, P1, K1]
            for out, taps in ((band1_hi, t["taps_hi"]), (band1_lo, t["taps_lo"])):
                ins = nc.gpsimd.tensor_tensor(
                    out[gslot][:, :, 0:P1 * K1].rearrange("p n (a j) -> p n a j", j=K1),
                    t["mask1"][:].rearrange("p (a j) -> p a j", j=K1).unsqueeze(1).broadcast_to(shape),
                    taps[:, bass.ds(g * n * K1, n * K1)].rearrange("p (n j) -> p n j", j=K1).unsqueeze(2).broadcast_to(shape),
                    ALU.mult)
            ins.then_inc(band1_built, 1)

        def group(g, gslot, last=False):
            def half(a, b):
                with pool.Fori(a // 2, b // 2) as m:
                    for k in range(2):
                        mix(g, 2 * m + k, QN * g + 2 * m + k, k, gslot)
            half(0, QN // 2)
            if not last:
                band1(g + 1, 1 - gslot)
            half(QN // 2, QN)

        band1(0, 0)
        for q in range(QN // 2):
            mix(0, q, q, q % 2, 0)
        band1(1, 1)
        for q in range(QN // 2, QN):
            mix(0, q, q, q % 2, 0)
        with pool.Fori(0, G // 2 - 1) as n:
            group(2 * n + 1, 1)
            group(2 * n + 2, 0)
        group(G - 1, 1, last=True)

    @block.vector
    def _(dve):
        def evac0(u, slot):
            for c in range(GC):
                dve.wait_ge(conv0_done, GC * u + c + 1)
                if not (known(u) and u < 2):
                    dve.wait_ge(normalised, u - 1)
                    dve.wait_ge(evac1_done, GC * (u - 2) + c + 1)
                dve.tensor_tensor(x1[slot][:, c, :, :], p0[c][:],
                                  t["shift"][:, bass.ds(IMAGES * u + UB * c, UB)].unsqueeze(2).broadcast_to([H, UB, W]),
                                  ALU.add).then_inc(evac0_done, 1)

        def stats(u, slot):
            dve.wait_ge(evac0_done, GC * u + GC)
            if not (known(u) and u < 1):
                dve.wait_ge(var_local, u)
            for b in range(UB):
                ins = dve.bn_stats(bnp[:, b, :], x1[slot][:, :, b, :])
            ins.then_inc(stats_local, 1)

        def about_mean(u):
            base = 2 * u
            dve.wait_ge(stats_local, u + 1)
            dve.wait_ge(mean_ready, u + 1)
            if not (known(u) and u < 1):
                dve.wait_ge(scales_ready, u)
            dve.tensor_copy(gm[:], pst[:, 0:UB])
            dve.tensor_tensor(dvp[:], bnp[:, :, 1:6:3], pst[:, 0:UB].unsqueeze(2).broadcast_to([H, UB, 2]),
                              ALU.subtract).then_inc(mean_chain, 1)
            dve.wait_ge(mean_chain, base + 1)
            dve.tensor_tensor(sqp[:], dvp[:], dvp[:], ALU.mult).then_inc(mean_chain, 1)
            dve.wait_ge(mean_chain, base + 2)
            dve.scalar_tensor_tensor(vap[:], bnp[:, :, 2:6:3], 2.0 / (GC * W), sqp[:], ALU.mult, ALU.add).then_inc(var_local, 1)

        def scales(u, slot):
            base = 5 * u
            dve.wait_ge(var_ready, u + 1)
            if not (known(u) and u < 2):
                dve.wait_ge(normalised, u - 1)
            dve.tensor_scalar(vare[:], pst[:, UB:2 * UB], EPS, None, ALU.add).then_inc(vare_ready, 1)
            dve.wait_ge(vare_ready, u + 1)
            dve.wait_ge(sd_ready, u + 1)
            dve.reciprocal(rs0[:], sd[:]).then_inc(scale_chain, 1)
            dve.wait_ge(scale_chain, base + 1)
            dve.tensor_tensor(n1[:], rs0[:], rs0[:], ALU.mult).then_inc(scale_chain, 1)
            dve.wait_ge(scale_chain, base + 2)
            dve.tensor_tensor(n2[:], n1[:], vare[:], ALU.mult).then_inc(scale_chain, 1)
            dve.wait_ge(scale_chain, base + 3)
            dve.tensor_scalar(n3[:], n2[:], -0.5 * SX, 1.5 * SX, ALU.mult, ALU.add).then_inc(scale_chain, 1)
            dve.wait_ge(scale_chain, base + 4)
            dve.tensor_tensor(rs1[slot][:], rs0[:], n3[:], ALU.mult).then_inc(scale_chain, 1)
            dve.wait_ge(scale_chain, base + 5)
            dve.scalar_tensor_tensor(nb1[slot][:], gm[:], -1.0, rs1[slot][:], ALU.mult, ALU.mult).then_inc(scales_ready, 1)

        def band0_build(u, slot):
            dve.wait_ge(taps0_ready, u + 1)
            if not (known(u) and u < 2):
                dve.wait_ge(conv0_done, GC * (u - 2) + GC)
            n = IMAGES * K0
            shape = [H, n, P0, K0]
            dve.tensor_tensor(band0[slot][:].rearrange("p n (a j) -> p n a j", j=K0),
                              t["mask0"][:].rearrange("p (a j) -> p a j", j=K0).unsqueeze(1).broadcast_to(shape),
                              pw[:, 0:n * K0].rearrange("p (n j) -> p n j", j=K0).unsqueeze(2).broadcast_to(shape),
                              ALU.mult).then_inc(band0_built, 1)

        def split(u, slot):
            dve.wait_ge(normalised, u + 1)
            if not (known(u) and u < 2):
                dve.wait_ge(conv1_done, GC * (u - 2) + GC)
            dve.tensor_tensor(lo[slot][:], norm[:], hi[slot][:], ALU.subtract).then_inc(split_done, 1)

        def evac1(u, slot, c):
            dve.wait_ge(conv1_done, GC * u + c + 1)
            if c == 0 and not (known(u) and u < 2):
                dve.wait_ge(stored[slot], 16 * GC // 2 * (u - slot))
            dve.scalar_tensor_tensor(y[slot][:, c, :, :], p1[c][:], 1.0 / (SX * SW), x1[slot][:, c, :, :],
                                     ALU.mult, ALU.add).then_inc(evac1_done, 1)

        band0_build(0, 0)
        band0_build(1, 1)
        evac0(0, 0)
        stats(0, 0)
        about_mean(0)
        scales(0, 0)
        split(0, 0)

        def step(g, q, u, slot, gslot):
            more = not (known(u) and u + 1 >= UNITS)
            if more:
                evac0(u + 1, 1 - slot)
                stats(u + 1, 1 - slot)
            if not (known(u) and u + 2 >= UNITS):
                band0_build(u + 2, slot)
            if more:
                about_mean(u + 1)
            evac1(u, slot, 0)
            if more:
                scales(u + 1, 1 - slot)
            evac1(u, slot, 1)
            if more:
                split(u + 1, 1 - slot)
            evac1(u, slot, 2)

        pairs(dve, step)

    @block.tensor
    def _(pe):
        def taps0(u, slot):
            pe.wait_ge(mixed, u + 1)
            if not (known(u) and u < 1):
                pe.wait_ge(band0_built, u)
            n = IMAGES * K0 * K0
            nc.tensor.matmul(pw[:, 0:n], t["classes"][:], wmix[slot][:], start=True, stop=True).then_inc(taps0_ready, 1)

        def conv0(u, slot):
            pe.wait_ge(centred, u + 1)
            pe.wait_ge(band0_built, u + 1)
            for c in range(GC):
                if not (known(u) and u < 1):
                    pe.wait_ge(evac0_done, GC * (u - 1) + c + 1)
                for b in range(UB):
                    for k, dx in enumerate((1, 0, 2)):
                        a, e = max(0, 1 - dx), W - max(0, dx - 1)
                        ins = nc.tensor.matmul(p0[c][:, b, a:e], band0[slot][:, (c * UB + b) * K0 + dx, 0:H],
                                               xt[slot][:, c, b, a + dx - 1:e + dx - 1],
                                               start=k == 0, stop=k == 2)
                ins.then_inc(conv0_done, 1)

        def conv1(u, slot, gslot, c):
            if not (known(u) and u < 1):
                pe.wait_ge(evac1_done, GC * (u - 1) + c + 1)
            half = K1 // 2
            order = [half] + [dx for dx in range(K1) if dx != half]
            for k, dx in enumerate(order):
                a, e = max(0, half - dx), W - max(0, dx - half)
                terms = ((band1_hi, hi), (band1_hi, lo), (band1_lo, hi))
                for m, (band, part) in enumerate(terms):
                    ins = nc.tensor.matmul(p1[c][:, :, a:e], band[gslot][:, c * K1 + dx, 0:H],
                                           part[slot][:, c, :, a + dx - half:e + dx - half],
                                           start=k == 0 and m == 0, stop=k == K1 - 1 and m == 2)
            ins.then_inc(conv1_done, 1)

        def mean(u):
            pe.wait_ge(stats_local, u + 1)
            for k in range(2):
                ins = nc.tensor.matmul(pst[:, 0:UB], t["average"][:], bnp[:, :, 1 + 3 * k], start=k == 0, stop=k == 1)
            ins.then_inc(mean_ready, 1)

        def var(u):
            pe.wait_ge(var_local, u + 1)
            for k in range(2):
                ins = nc.tensor.matmul(pst[:, UB:2 * UB], t["average"][:], vap[:, :, k], start=k == 0, stop=k == 1)
            ins.then_inc(var_ready, 1)

        taps0(0, 0)
        taps0(1, 1)
        conv0(0, 0)
        mean(0)
        var(0)

        def step(g, q, u, slot, gslot):
            more = not (known(u) and u + 1 >= UNITS)
            if not (known(u) and u + 2 >= UNITS):
                taps0(u + 2, slot)
            if more:
                conv0(u + 1, 1 - slot)
            pe.wait_ge(split_done, u + 1)
            pe.wait_ge(normalised, u + 1)
            pe.wait_ge(band1_built, g + 1)
            conv1(u, slot, gslot, 0)
            if more:
                mean(u + 1)
            conv1(u, slot, gslot, 1)
            if more:
                var(u + 1)
            conv1(u, slot, gslot, 2)

        pairs(pe, step)


def build(nc, d):
    with ExitStack() as ctx:
        def sem(name):
            return ctx.enter_context(nc.semaphore(name))

        def sb(name, shape, dt=F32):
            return ctx.enter_context(nc.sbuf_tensor(name, shape, dt))

        d["xs"] = d["x"].rearrange("b c h w -> b c (h w)")
        d["x_units"] = d["x"].rearrange("(q b) (g c) h w -> g q c b h w", b=UB, c=GC)
        d["out_units"] = d["out"].rearrange("(q b) (g c) h w -> g q c b h w", b=UB, c=GC)
        t = {
            "negmean": sb("negmean", [H, G * B]),
            "shift": sb("shift", [H, UNITS * IMAGES]),
            "hidden": sb("hidden", [C, G, B]),
            "w2rot": sb("w2rot", [C, C * K0 * K0]),
            "taps_hi": sb("taps_hi", [H, C * K1 * K1], F16),
            "taps_lo": sb("taps_lo", [H, C * K1 * K1], F16),
            "mask0": sb("mask0", [H, W0]),
            "mask1": sb("mask1", [H, P1 * K1], F16),
            "classes": sb("classes", [C, H]),
            "average": sb("average", [H, H]),
            "ones_set": sem("ones_set"),
        }
        with ExitStack() as inner:
            statistics_block(nc, inner, t, d, sem)
        with ExitStack() as inner:
            main_block(nc, inner, t, d, sem)


def constants():
    import numpy as np

    p = np.arange(H)
    c = np.arange(C)
    k = c % 32
    out = {
        "group_sum": (c[:, None] // GC == c[None, :] // GC).astype(np.float32),
        "first_of_group": (c[:, None] == GC * np.arange(G)[None, :]).astype(np.float32),
        "classes": (c[:, None] // 32 == p[None, :] % K0).astype(np.float32),
    }
    h = np.arange(W0)
    out["mask0"] = ((abs(h[None, :] - p[:, None]) <= K0 // 2) & (h[None, :] < H)).astype(np.float32)
    h = np.arange(P1 * K1)
    out["mask1"] = ((abs(h[None, :] - p[:, None]) <= K1 // 2) & (h[None, :] < H)).astype(np.float16)
    j = np.arange(K1)
    out["y0"] = ((p[:, None] - j[None, :] + K1 // 2) % K1 - K1 // 2).astype(np.float32)
    out["y1"] = np.broadcast_to((j - K1 // 2).astype(np.float32), (H, K1)).copy()
    out["ones_k"] = np.stack([k < RED, k == RED, k == RED + 1], 1).astype(np.float32)
    return out


def kernel(x, L0_conv_w1, L0_conv_gamma, L0_conv_beta, L0_conv_running_mean, L0_conv_running_var,
           L0_conv_w2, L0_conv_b2, L0_conv_bias, L1_conv_diff_metric):
    import numpy as np
    import concourse.bacc as bacc
    from concourse.bass_utils import run_bass_kernel_spmd as run

    f = np.float32
    con = constants()
    w1rep = np.zeros((C, K0, 32), f)
    w1rep[:, :, 0:RED] = np.asarray(L0_conv_w1).T[:, None, :]
    vec = np.zeros((K0, 32, 7), f)
    vec[:, :, 3] = 1.0
    for n, v in enumerate((L0_conv_gamma, L0_conv_beta, L0_conv_running_mean, L0_conv_running_var)):
        vec[:, 0:RED, n] = np.asarray(v)[None, :]
    vec[:, :, 4:7] = con.pop("ones_k").reshape(K0, 32, 3)
    w2 = np.asarray(L0_conv_w2).reshape(C, K0, K0, RED)
    b2 = np.asarray(L0_conv_b2).reshape(C, K0, K0)
    w2rot = np.zeros((K0, 32, C, K0, K0), f)
    for r in range(K0):
        for j in range(K0):
            dy = (r - j + 1) % K0
            w2rot[r, 0:RED, :, :, j] = w2[:, dy, :, :].transpose(2, 0, 1)
            w2rot[r, RED, :, :, j] = b2[:, dy, :]
            if dy == 1:
                w2rot[r, RED + 1, :, 1, j] = 1.0
    arrays = {
        "x": np.ascontiguousarray(x),
        "w1rep": w1rep.reshape(C, C),
        "bnvec": vec.reshape(C, 7),
        "w2rot": w2rot.reshape(C, C * K0 * K0),
        "biasb": np.broadcast_to(np.asarray(L0_conv_bias), (H, C)).copy(),
        "dm": np.broadcast_to(np.asarray(L1_conv_diff_metric).reshape(C, 4), (H, C, 4)).copy(),
        **con,
    }
    nc = bacc.Bacc("TRN2", target_bir_lowering=False, num_devices=1)
    d = {n: nc.dram_tensor(f"in_{n}_dram", a.shape, mybir.dt.from_np(a.dtype), kind="ExternalInput").ap()
         for n, a in arrays.items()}
    d["out"] = nc.dram_tensor("out_0_dram", (B, C, H, W), F32, kind="ExternalOutput").ap()
    build(nc, d)
    r = run(nc, [{f"in_{n}_dram": a for n, a in arrays.items()}], core_ids=[0])
    return r.results[0]["out_0_dram"]
```

```python
from contextlib import ExitStack
import math

import concourse.bass as bass
from concourse import mybir

F32 = mybir.dt.float32
F16 = mybir.dt.float16
ALU = mybir.AluOpType
ACT = mybir.ActivationFunctionType
AX = mybir.AxisListType

B, C, H, W = 32, 96, 128, 128
G = 32
GC = C // G
IMG = H * W
RED = C // 4
EPS = 1e-5

QB = 4
QUADS = B // QB
XB = 8
XCHUNKS = B // XB
BANK = 512

K0 = 3
P0 = -(-H // K0)
W0 = P0 * K0

K1 = 9
REACH = K1 // 2
STRIPS = 4
SR = H // STRIPS
TR, TCOL = 16, 8
HALVES = SR // TR
TILES = W // TCOL
OR, OC = TR + K1 - 1, TCOL + K1 - 1
BC = BANK // TR
BANKS = HALVES * W // BC
FILL = 4
FILLS = HALVES * TILES // FILL
NC = BC
NCHUNKS = W // NC
SUBS = SR * W // 512
PADDED = H + 2 * B

LOOP = 6
TURNS = C // LOOP
LEAD = 6

SX = 2.0 ** 8
SW = 2.0 ** 16

ALPHA = 0.65
C1 = 1.0 / math.gamma(1.0 + 1.0 / ALPHA)
C2 = math.sqrt(2.0 * C1)
VAL = 3.0 * (-2.0 + (1.0 + 2.0 * ALPHA) * C2) / ((1.0 + 2.0 * ALPHA) * (-2.0 * C1 + 3.0 * C2))
GAUSS = VAL / (4.0 * math.pi * C1)
POISSON = (1.0 - VAL) * math.gamma(1.5) / math.pi ** 1.5 * C2

CHUNKS = 4
CHUNK = IMG // CHUNKS
BN = 512
STATS = CHUNK // BN


def statistics_block(nc, ctx, t, d, sem):
    def sb(name, shape, dt=F32):
        return ctx.enter_context(nc.sbuf_tensor(name, shape, dt))

    piece = [sb(f"piece{i}", [C, CHUNK]) for i in range(CHUNKS)]
    bn = sb("bn", [C, B, CHUNKS * STATS, 6])
    mv = sb("mv", [C, B, 2])
    small = {n: sb(n, [C, B]) for n in ("gmean", "dev", "var", "vare", "sd", "rs", "t1", "t2", "pooled", "hlin", "hsig", "hm")}
    col = {n: sb(n, [C, 1]) for n in ("rve", "rsd", "rr", "c1", "c2", "bnscale")}
    group_sum = sb("group_sum", [C, C])
    w1rep = sb("w1rep", [C, C])
    bnvec = sb("bnvec", [C, 7])
    first_of_group = sb("first_of_group", [C, G])
    wide = sb("wide", [C, G, B])
    ones = sb("ones", [C, H])

    ps = ctx.enter_context(nc.psum_tensor("ps_small", [H, 512], F32))
    pwide = ctx.enter_context(nc.psum_tensor("ps_wide", [H, 2, 512], F32))

    piece_loaded = [sem(f"piece_loaded{i}") for i in range(CHUNKS)]
    piece_read = sem("piece_read")
    consts_loaded = sem("consts_loaded")
    chain = sem("vector_chain")
    psum_ready = sem("psum_ready")
    to_psum = sem("to_psum")
    ones_set = sem("ones_set")
    to_act = sem("to_act")
    act_done = sem("act_done")

    block = ctx.enter_context(nc.Block())

    @block.sync
    def _(sp):
        for dst, src in ((group_sum, d["group_sum"]), (w1rep, d["w1rep"]), (bnvec, d["bnvec"]),
                         (first_of_group, d["first_of_group"]),
                         *((t[n], d[n]) for n in ("biasb", "dm", "y0", "y1", "mask0", "mask1", "classes",
                                                  "w2rot", "average", "ident"))):
            sp.dma_start(dst[:], src).then_inc(consts_loaded, 16)
        for i in range(CHUNKS):
            sp.dma_start(piece[i][:], d["xs"][0, :, i * CHUNK:(i + 1) * CHUNK]).then_inc(piece_loaded[i], 16)
        with sp.Fori(1, B) as b:
            for i in range(CHUNKS):
                sp.wait_ge(piece_read, CHUNKS * (b - 1) + i + 1)
                sp.dma_start(piece[i][:], d["xs"][bass.ds(b, 1), :, i * CHUNK:(i + 1) * CHUNK]
                             .rearrange("a c n -> (a c) n")).then_inc(piece_loaded[i], 16)

    @block.vector
    def _(dve):
        count = [0]

        def link(ins):
            count[0] += 1
            ins.then_inc(chain, 1)
            dve.wait_ge(chain, count[0])

        with dve.Fori(0, B) as b:
            for i in range(CHUNKS):
                dve.wait_ge(piece_loaded[i], 16 * b + 16)
                for j in range(STATS):
                    ins = dve.bn_stats(bn[:, bass.ds(b, 1), i * STATS + j, :].rearrange("c a s -> c (a s)"),
                                       piece[i][:, j * BN:(j + 1) * BN])
                ins.then_inc(piece_read, 1)
        dve.wait_ge(piece_read, B * CHUNKS)
        for b in range(B):
            ins = dve.bn_aggr(mv[:, b, :], bn[:, b, :, :].rearrange("c n s -> c (n s)"))
        link(ins)
        s = small
        dve.tensor_copy(s["t1"][:], mv[:, :, 0]).then_inc(to_psum, 1)
        dve.wait_ge(psum_ready, 1)
        link(dve.tensor_scalar(s["gmean"][:], ps[0:C, 0:B], 1.0 / GC, None, ALU.mult))
        link(dve.tensor_tensor(s["dev"][:], mv[:, :, 0], s["gmean"][:], ALU.subtract))
        link(dve.tensor_tensor(s["t2"][:], s["dev"][:], s["dev"][:], ALU.mult))
        dve.tensor_tensor(s["var"][:], s["t2"][:], mv[:, :, 1], ALU.add).then_inc(to_psum, 1)
        dve.wait_ge(psum_ready, 2)
        dve.tensor_scalar(s["vare"][:], ps[0:C, B:2 * B], 1.0 / GC, EPS, ALU.mult, ALU.add).then_inc(to_act, 1)
        dve.wait_ge(act_done, 1)
        link(dve.reciprocal(s["rs"][:], s["sd"][:]))
        link(dve.tensor_tensor(s["t1"][:], s["rs"][:], s["rs"][:], ALU.mult))
        link(dve.tensor_tensor(s["t2"][:], s["t1"][:], s["vare"][:], ALU.mult))
        link(dve.tensor_scalar(s["t1"][:], s["t2"][:], -0.5, 1.5, ALU.mult, ALU.add))
        link(dve.tensor_tensor(s["hm"][:], s["rs"][:], s["t1"][:], ALU.mult))
        link(dve.tensor_copy(s["rs"][:], s["hm"][:]))
        dve.tensor_tensor(s["pooled"][:], s["dev"][:], s["rs"][:], ALU.mult).then_inc(to_psum, 1)
        dve.wait_ge(consts_loaded, 16 * 14)
        dve.tensor_scalar(col["rve"][:], bnvec[:, 3:4], EPS, None, ALU.add).then_inc(to_act, 1)
        dve.wait_ge(act_done, 2)
        link(dve.reciprocal(col["rr"][:], col["rsd"][:]))
        link(dve.tensor_tensor(col["c1"][:], col["rr"][:], col["rr"][:], ALU.mult))
        link(dve.tensor_tensor(col["c2"][:], col["c1"][:], col["rve"][:], ALU.mult))
        link(dve.tensor_scalar(col["c1"][:], col["c2"][:], -0.5, 1.5, ALU.mult, ALU.add))
        link(dve.tensor_tensor(col["c2"][:], col["rr"][:], col["c1"][:], ALU.mult))
        link(dve.tensor_tensor(col["bnscale"][:], col["c2"][:], bnvec[:, 0:1], ALU.mult))
        dve.wait_ge(psum_ready, 3)
        dve.tensor_scalar(s["hlin"][:], ps[0:C, 2 * B:3 * B], bnvec[:, 2:3], col["bnscale"][:, 0:1],
                          ALU.subtract, ALU.mult).then_inc(to_act, 1)
        dve.wait_ge(act_done, 3)
        link(dve.tensor_scalar(s["hm"][:], s["hsig"][:], bnvec[:, 4:5], bnvec[:, 5:6], ALU.mult, ALU.add))
        fog = first_of_group[:].unsqueeze(2).broadcast_to([C, G, B])
        dve.tensor_tensor(wide[:], fog, s["gmean"][:].unsqueeze(1).broadcast_to([C, G, B]), ALU.mult).then_inc(to_psum, 1)
        dve.wait_ge(psum_ready, 4)
        pw = pwide[:].rearrange("p a n -> p (a n)")
        link(dve.tensor_scalar(t["negmean"][:], pw, -1.0, None, ALU.mult))
        dve.tensor_tensor(wide[:], fog, s["rs"][:].unsqueeze(1).broadcast_to([C, G, B]), ALU.mult).then_inc(to_psum, 1)
        dve.wait_ge(psum_ready, 5)
        link(dve.tensor_tensor(t["hidden"][:], pw[0:C, :].rearrange("p (g b) -> p g b", b=B),
                               s["hm"][:].unsqueeze(1).broadcast_to([C, G, B]), ALU.mult))
        hid = t["hidden"][:].rearrange("p g b -> p (g b)")
        link(dve.tensor_scalar(hid, hid, bnvec[:, 6:7], None, ALU.add))

    @block.scalar
    def _(act):
        act.wait_ge(to_act, 1)
        nc.scalar.activation(small["sd"][:], small["vare"][:], ACT.Sqrt).then_inc(act_done, 1)
        act.wait_ge(to_act, 2)
        nc.scalar.activation(col["rsd"][:], col["rve"][:], ACT.Sqrt).then_inc(act_done, 1)
        act.wait_ge(to_act, 3)
        nc.scalar.activation(small["hsig"][:], small["hlin"][:], ACT.Sigmoid, bias=bnvec[:, 1:2]).then_inc(act_done, 1)

    @block.gpsimd
    def _(pool):
        nc.gpsimd.memset(ones[:], 1.0).then_inc(ones_set, 1)

    @block.tensor
    def _(pe):
        pe.wait_ge(consts_loaded, 16 * 14)
        pe.wait_ge(ones_set, 1)
        steps = ((group_sum, small["t1"], 0), (group_sum, small["var"], B), (w1rep, small["pooled"], 2 * B))
        for n, (lhs, rhs, at) in enumerate(steps):
            pe.wait_ge(to_psum, n + 1)
            nc.tensor.matmul(ps[0:C, at:at + B], lhs[:], rhs[:], start=True, stop=True).then_inc(psum_ready, 1)
        for n in range(2):
            pe.wait_ge(to_psum, 4 + n)
            for a in range(2):
                ins = nc.tensor.matmul(pwide[:, a, :], ones[:], wide[:].rearrange("c g b -> c (g b)")[:, a * 512:(a + 1) * 512],
                                       start=True, stop=True)
            ins.then_inc(psum_ready, 1)


def main_block(nc, ctx, t, d, sem):
    def sb(name, shape, dt=F32):
        return ctx.enter_context(nc.sbuf_tensor(name, shape, dt))

    xt = [sb(f"xt{k}", [H, XB, W]) for k in range(XCHUNKS)]
    band0 = [sb(f"band0_{i}", [H, QB * K0, W0]) for i in range(2)]
    wmix = [sb(f"wmix{i}", [C, B * K0 * K0]) for i in range(2)]
    wrow = [sb(f"wrow{i}", [H, B * K0 * K0]) for i in range(2)]
    x1row = sb("x1row", [H, B, W])
    strip = [sb(f"strip{j}", [H, SR, W]) for j in range(LOOP)]
    norm = [sb(f"norm{i}", [H, NC // TCOL, SR, TCOL]) for i in range(2)]
    tile_hi = sb("tile_hi", [H, HALVES * TILES, PADDED], F16)
    tile_lo = sb("tile_lo", [H, HALVES * TILES, PADDED], F16)
    taps_hi = [sb(f"taps_hi{i}", [H, OC, OR], F16) for i in range(2)]
    taps_lo = [sb(f"taps_lo{i}", [H, OC, OR], F16) for i in range(2)]
    zr = [sb(f"zr{i}", [H, OR]) for i in range(2)]
    zc = [sb(f"zc{i}", [H, OC]) for i in range(2)]
    za, zb, zd, ze = (sb(n, [H, OC * OR]) for n in ("za", "zb", "zd", "ze"))
    bnp = sb("bnp", [H, GC * SUBS, 6])
    n_sub = GC * SUBS
    dvp = sb("dvp", [H, n_sub, 2])
    sqp = sb("sqp", [H, n_sub, 2])
    vap = sb("vap", [H, n_sub, 2])
    col = {n: sb(n + "1", [H, 1]) for n in ("msum", "vsum", "gm", "vare", "sd", "rs", "s1", "s2", "s3")}
    scale = [sb(f"scale{i}", [H, 1]) for i in range(2)]
    offset = [sb(f"offset{i}", [H, 1]) for i in range(2)]

    def psum(name, shape):
        return ctx.enter_context(nc.psum_tensor(name, shape, F32))

    p0 = [psum(f"p0_{i}", [H, QB, W]) for i in range(2)]
    pt = [psum(f"pt{i}", [H, FILL, H]) for i in range(2)]
    p1 = [psum(f"p1_{i}", [H, BC, TR]) for i in range(2)]
    pw = psum("pw", [H, BANK])
    pst = psum("pst", [H, BANK])

    x_loaded = [sem(f"x_loaded{k}") for k in range(XCHUNKS)]
    centred = sem("centred")
    mixed = sem("mixed")
    taps0_ready = sem("taps0_ready")
    wrow_copied = sem("wrow_copied")
    band0_built = sem("band0_built")
    conv0_quad = sem("conv0_quad")
    evac0_done = sem("evac0_done")
    stripped = sem("stripped")
    bn_done = sem("bn_done")
    mean_local = sem("mean_local")
    mean_ready = sem("mean_ready")
    mean_chain = sem("mean_chain")
    var_sum = sem("var_sum")
    var_local = sem("var_local")
    var_ready = sem("var_ready")
    vare_ready = sem("vare_ready")
    sd_ready = sem("sd_ready")
    scale_chain = sem("scale_chain")
    scales_ready = sem("scales_ready")
    norm_done = sem("norm_done")
    turned = sem("turned")
    hi_done = sem("hi_done")
    lo_done = sem("lo_done")
    pads_zero = sem("pads_zero")
    r2_chain = sem("r2_chain")
    r2_ready = sem("r2_ready")
    s_ready = sem("s_ready")
    root_ready = sem("root_ready")
    taps_chain = sem("taps_chain")
    conv1_bank = sem("conv1_bank")
    evac1_done = sem("evac1_done")
    stored = [sem(f"stored{j}") for j in range(LOOP)]

    block = ctx.enter_context(nc.Block())

    def tiles_of(f):
        first = f % HALVES * TILES + f // HALVES * FILL
        return slice(first, first + FILL)

    def banks_over(f):
        return HALVES * min(f // HALVES + 2, W // BC)

    def known(v):
        return isinstance(v, int)

    class Unit:

        def __init__(self, turn, j):
            self.turn, self.j = turn + j // LOOP, j % LOOP
            self.u = LOOP * self.turn + self.j
            self.slot = self.j % 2
            self.c = self.j % GC
            self.group = LOOP // GC * self.turn + self.j // GC
            self.gslot = self.j // GC % 2
            self.real = not known(self.u) or 0 <= self.u < C

    def need(eng, s, value):
        if not known(value) or value > 0:
            eng.wait_ge(s, value)

    def units(eng, step):
        for j in range(-LEAD, LOOP):
            step(j // LOOP, j % LOOP)
        with eng.Fori(1, TURNS - 1) as turn:
            for j in range(LOOP):
                now = eng.alloc_register(f"turn_of_step{j}")
                eng.reg_mov(now, turn)
                step(eng.snap(now, min_val=1, max_val=TURNS - 2), j)
        for j in range(LOOP):
            step(TURNS - 1, j)

    @block.sync
    def _(sp):
        def load(v):
            for k in range(XCHUNKS):
                need(sp, conv0_quad, QUADS * (v.u - 1) + XB // QB * (k + 1))
                src = d["x_rows"][bass.ds(v.u, 1), :, XB * k:XB * (k + 1), :]
                sp.dma_start(xt[k][:], src.rearrange("a h b w -> h (a b) w")).then_inc(x_loaded[k], 16)

        def store(v):
            need(sp, evac1_done, BANKS * (v.u + 1))
            for q in range(STRIPS):
                dst = d["out_strips"][bass.ds(v.u, 1), q, :, :]
                sp.dma_start(dst.rearrange("a b n -> (a b) n"),
                             strip[v.j][B * q:B * (q + 1), :, :].rearrange("p r w -> p (r w)")).then_inc(stored[v.j], 16)

        def step(turn, j):
            a, o = Unit(turn, j), Unit(turn, j + 6)
            if o.real:
                load(o)
            if a.real:
                store(a)

        units(sp, step)
        for s in stored:
            sp.wait_ge(s, 16 * STRIPS * TURNS)

    @block.scalar
    def _(act):
        def centre(v, k):
            need(act, x_loaded[k], 16 * (v.u + 1))
            for b in range(XB):
                ins = nc.scalar.activation(xt[k][:, b, :], xt[k][:, b, :], ACT.Identity,
                                           bias=t["negmean"][:, bass.ds(B * v.group + XB * k + b, 1)])
            ins.then_inc(centred, 1)

        def root(v):
            need(act, vare_ready, v.group + 1)
            nc.scalar.activation(col["sd"][:], col["vare"][:], ACT.Sqrt).then_inc(sd_ready, 1)

        def normalise(v, k):
            need(act, scales_ready, v.group + 1)
            need(act, turned, FILLS * v.u + HALVES * (k - 1))
            nc.scalar.activation(norm[k % 2][:].rearrange("p i r s -> p r i s"),
                                 strip[v.j][:, :, NC * k:NC * (k + 1)].rearrange("p r (i s) -> p r i s", s=TCOL),
                                 ACT.Identity, bias=offset[v.gslot][:, 0:1],
                                 scale=scale[v.gslot][:, 0:1]).then_inc(norm_done, 1)

        def high(v, f):
            need(act, turned, FILLS * v.u + f + 1)
            need(act, conv1_bank, BANKS * (v.u - 1) + banks_over(f))
            nc.scalar.activation(tile_hi[:, tiles_of(f), B:B + H], pt[f % 2][:], ACT.Copy).then_inc(hi_done, 1)

        def tap_parts(v):
            need(act, s_ready, v.u + 1)
            nc.scalar.activation(zb[:], za[:], ACT.Sqrt).then_inc(root_ready, 1)
            need(act, taps_chain, 9 * v.u)
            nc.scalar.activation(ze[:], zd[:], ACT.Exp, scale=-1.0 / (4.0 * C1)).then_inc(root_ready, 1)

        def step(turn, j):
            a, n, w, o = Unit(turn, j), Unit(turn, j + 1), Unit(turn, j + 5), Unit(turn, j + 6)
            if a.real:
                high(a, 4)
                high(a, 5)
            if w.real:
                centre(w, 2)
            if a.real:
                high(a, 6)
                high(a, 7)
            if w.real:
                centre(w, 3)
            if n.real:
                if j % GC == GC - 1:
                    root(n)
                tap_parts(n)
                normalise(n, 0)
                normalise(n, 1)
                high(n, 0)
                high(n, 1)
            if o.real:
                centre(o, 0)
            if n.real:
                normalise(n, 2)
                high(n, 2)
                high(n, 3)
            if o.real:
                centre(o, 1)
            if n.real:
                normalise(n, 3)

        units(act, step)

    @block.gpsimd
    def _(pool):
        def mix(v):
            need(pool, taps0_ready, v.u - 1)
            shape = [C, B, K0 * K0]
            w2c = t["w2rot"][:, bass.ds(K0 * K0 * v.u, K0 * K0)]
            hid = t["hidden"][:].rearrange("k g b -> k (g b)")[:, bass.ds(B * v.group, B)]
            nc.gpsimd.tensor_tensor(wmix[v.slot][:].rearrange("k (b r) -> k b r", b=B),
                                    w2c.unsqueeze(1).broadcast_to(shape),
                                    hid.unsqueeze(2).broadcast_to(shape), ALU.mult).then_inc(mixed, 1)

        def band(v, q):
            need(pool, wrow_copied, v.u + 1)
            need(pool, conv0_quad, QUADS * v.u + q - 1)
            n = QB * K0
            shape = [H, n, P0, K0]
            taps = wrow[v.slot][:, q * n * K0:(q + 1) * n * K0].rearrange("p (n j) -> p n j", j=K0)
            nc.gpsimd.tensor_tensor(band0[q % 2][:].rearrange("p n (a j) -> p n a j", j=K0),
                                    t["mask0"][:].rearrange("p (a j) -> p a j", j=K0).unsqueeze(1).broadcast_to(shape),
                                    taps.unsqueeze(2).broadcast_to(shape), ALU.mult).then_inc(band0_built, 1)

        def distance(v):
            base = 6 * v.u
            full = [H, OC, OR]

            def entry(i, n):
                return t["dm"][:, bass.ds(4 * v.u + i, 1)].broadcast_to([H, n])

            need(pool, r2_ready, v.u)
            for i in range(2):
                nc.gpsimd.tensor_tensor(zr[i][:], entry(2 * i, OR), t["y0"][:], ALU.mult)
                ins = nc.gpsimd.tensor_tensor(zc[i][:], entry(2 * i + 1, OC), t["y1"][:], ALU.mult)
                ins.then_inc(r2_chain, 1)
            need(pool, taps_chain, 9 * v.u)
            for i, z in enumerate((za, zd)):
                need(pool, r2_chain, base + 2 + i)
                nc.gpsimd.tensor_tensor(z[:].rearrange("p (x y) -> p x y", x=OC), zr[i][:].unsqueeze(1).broadcast_to(full),
                                        zc[i][:].unsqueeze(2).broadcast_to(full), ALU.add).then_inc(r2_chain, 1)
            for i, z in enumerate((za, zd)):
                need(pool, r2_chain, base + 3 + i)
                nc.gpsimd.tensor_tensor(z[:], z[:], z[:], ALU.mult).then_inc(r2_chain, 1)
            need(pool, r2_chain, base + 6)
            nc.gpsimd.tensor_tensor(zd[:], za[:], zd[:], ALU.add).then_inc(r2_ready, 1)

        def step(turn, j):
            n, w, o = Unit(turn, j + 1), Unit(turn, j + 5), Unit(turn, j + 6)
            for q in range(QUADS):
                if w.real:
                    band(w, q)
                if q == 1 and n.real:
                    distance(n)
                if q == 2 and o.real:
                    mix(o)

        units(pool, step)

    @block.vector
    def _(dve):
        def copy_wrow(v):
            need(dve, taps0_ready, v.u + 1)
            need(dve, band0_built, QUADS * (v.u - 1))
            dve.tensor_copy(wrow[v.slot][:], pw[:, 0:B * K0 * K0]).then_inc(wrow_copied, 1)

        def evac0(v, q):
            need(dve, conv0_quad, QUADS * v.u + q + 1)
            if q == 0:
                need(dve, stripped, XCHUNKS * v.u)
            mean = t["negmean"][:, bass.ds(B * v.group + QB * q, QB)].unsqueeze(2).broadcast_to([H, QB, W])
            dve.scalar_tensor_tensor(x1row[:, QB * q:QB * (q + 1), :], p0[q % 2][:], t["biasb"][:, bass.ds(v.u, 1)],
                                     mean, ALU.add, ALU.subtract).then_inc(evac0_done, 1)

        def turn_rows(v, i):
            if i == 0:
                need(dve, evac0_done, QUADS * (v.u + 1))
                need(dve, stored[v.j], 16 * STRIPS * v.turn)
            cols = slice(W // XCHUNKS * i, W // XCHUNKS * (i + 1))
            dve.transpose(strip[v.j][:, :, cols].rearrange("p r w -> p w r"),
                          x1row[:, :, cols].rearrange("p b w -> p w b")).then_inc(stripped, 1)

        def stats(v, i):
            if i == 0:
                need(dve, stripped, XCHUNKS * (v.u + 1))
                if v.c == 0:
                    need(dve, var_local, v.group)
            rows = SR // SUBS
            dve.bn_stats(bnp[:, SUBS * v.c + i, :], strip[v.j][:, rows * i:rows * (i + 1), :]
                         .rearrange("p r w -> p (r w)")).then_inc(bn_done, 1)

        def local_mean(v):
            need(dve, bn_done, SUBS * GC * (v.group + 1))
            need(dve, mean_ready, v.group)
            dve.tensor_reduce(col["msum"][:], bnp[:, :, 1:6:3], AX.XY, ALU.add).then_inc(mean_local, 1)

        def local_var(v):
            base = 3 * v.group
            need(dve, mean_ready, v.group + 1)
            need(dve, scales_ready, v.group)
            dve.tensor_copy(col["gm"][:], pst[:, 0:1]).then_inc(mean_chain, 1)
            need(dve, mean_chain, base + 1)
            dve.tensor_scalar(dvp[:], bnp[:, :, 1:6:3], col["gm"][:, 0:1], None, ALU.subtract).then_inc(mean_chain, 1)
            need(dve, mean_chain, base + 2)
            dve.tensor_tensor(sqp[:], dvp[:], dvp[:], ALU.mult).then_inc(mean_chain, 1)
            need(dve, mean_chain, base + 3)
            dve.scalar_tensor_tensor(vap[:], bnp[:, :, 2:6:3], 2.0 / BANK, sqp[:], ALU.mult, ALU.add).then_inc(var_sum, 1)
            need(dve, var_sum, v.group + 1)
            dve.tensor_reduce(col["vsum"][:], vap[:], AX.XY, ALU.add).then_inc(var_local, 1)

        def scales(v, part):
            base = 5 * v.group
            if part == 0:
                need(dve, var_ready, v.group + 1)
                dve.tensor_scalar(col["vare"][:], pst[:, 1:2], EPS, None, ALU.add).then_inc(vare_ready, 1)
                return
            need(dve, vare_ready, v.group + 1)
            need(dve, sd_ready, v.group + 1)
            dve.reciprocal(col["rs"][:], col["sd"][:]).then_inc(scale_chain, 1)
            need(dve, scale_chain, base + 1)
            dve.tensor_tensor(col["s1"][:], col["rs"][:], col["rs"][:], ALU.mult).then_inc(scale_chain, 1)
            need(dve, scale_chain, base + 2)
            dve.tensor_tensor(col["s2"][:], col["s1"][:], col["vare"][:], ALU.mult).then_inc(scale_chain, 1)
            need(dve, scale_chain, base + 3)
            dve.tensor_scalar(col["s3"][:], col["s2"][:], -0.5 * SX, 1.5 * SX, ALU.mult, ALU.add).then_inc(scale_chain, 1)
            need(dve, scale_chain, base + 4)
            need(dve, norm_done, NCHUNKS * GC * (v.group - 1))
            dve.tensor_tensor(scale[v.gslot][:], col["rs"][:], col["s3"][:], ALU.mult).then_inc(scale_chain, 1)
            need(dve, scale_chain, base + 5)
            dve.scalar_tensor_tensor(offset[v.gslot][:], col["gm"][:], -1.0, scale[v.gslot][:], ALU.mult,
                                     ALU.mult).then_inc(scales_ready, 1)

        def low(v, f):
            need(dve, hi_done, FILLS * v.u + f + 1)
            need(dve, conv1_bank, BANKS * (v.u - 1) + banks_over(f))
            dve.tensor_tensor(tile_lo[:, tiles_of(f), B:B + H], pt[f % 2][:], tile_hi[:, tiles_of(f), B:B + H],
                              ALU.subtract).then_inc(lo_done, 1)

        def tap_sum(v):
            need(dve, r2_ready, v.u + 1)
            dve.tensor_scalar(za[:], zd[:], C2 * C2, None, ALU.add).then_inc(s_ready, 1)

        def taps1(v, first, last):
            base = 9 * v.u
            taps_h = taps_hi[v.slot][:].rearrange("p x y -> p (x y)")
            taps_l = taps_lo[v.slot][:].rearrange("p x y -> p (x y)")
            steps = (
                lambda: dve.reciprocal(zd[:], zb[:]),
                lambda: dve.tensor_tensor(zd[:], zd[:], za[:], ALU.mult),
                lambda: dve.tensor_tensor(zb[:], zb[:], zd[:], ALU.add),
                lambda: dve.tensor_tensor(zb[:], zb[:], za[:], ALU.mult),
                lambda: dve.reciprocal(zd[:], zb[:]),
                lambda: dve.scalar_tensor_tensor(ze[:], ze[:], GAUSS / (2.0 * POISSON), zd[:], ALU.mult, ALU.add),
                lambda: dve.scalar_tensor_tensor(zb[:], ze[:], 2.0 * POISSON * SW, t["mask1"][:], ALU.mult, ALU.mult),
                lambda: dve.tensor_copy(taps_h, zb[:]),
                lambda: dve.tensor_tensor(taps_l, zb[:], taps_h, ALU.subtract),
            )
            for k in range(first, last):
                if k == 0:
                    need(dve, root_ready, 2 * v.u + 2)
                need(dve, taps_chain, base + k)
                steps[k]().then_inc(taps_chain, 1)

        def evac1(v, i):
            need(dve, conv1_bank, BANKS * v.u + i + 1)
            w, h = divmod(i, HALVES)
            part = strip[v.j][:, TR * h:TR * (h + 1), BC * w:BC * (w + 1)]
            dve.scalar_tensor_tensor(part, p1[i % 2][:].rearrange("p c r -> p r c"), 1.0 / (SX * SW), part,
                                     ALU.mult, ALU.add).then_inc(evac1_done, 1)

        for z in (tile_hi, tile_lo):
            dve.memset(z[:, :, 0:B], 0.0)
            ins = dve.memset(z[:, :, B + H:PADDED], 0.0)
        ins.then_inc(pads_zero, 1)

        stats_by = (0, 0, 0, 2, 4, 5, 6, 7, 8)
        taps1_by = (0, 0, 0, 0, 1, 4, 5, 7, 9)

        def step(turn, j):
            a, n, m = Unit(turn, j), Unit(turn, j + 1), Unit(turn, j + 4)
            w, o = Unit(turn, j + 5), Unit(turn, j + 6)
            scaling = j % GC == GC - 1 and n.real
            if scaling:
                local_mean(n)
            if a.real:
                low(a, 4)
                low(a, 5)
            if m.real:
                turn_rows(m, 0)
                turn_rows(m, 1)
            if a.real:
                evac1(a, 0)
            if m.real:
                turn_rows(m, 2)
                turn_rows(m, 3)
            for i in range(BANKS):
                if i == 1 and a.real:
                    low(a, 6)
                    low(a, 7)
                if i == 2 and n.real:
                    tap_sum(n)
                if i == 3 and scaling:
                    scales(n, 1)
                if i > 0 and a.real:
                    evac1(a, i)
                if w.real:
                    evac0(w, i)
                if i == 0 and scaling:
                    local_var(n)
                if i == 1 and scaling:
                    scales(n, 0)
                if i == 4 and n.real:
                    low(n, 0)
                    low(n, 1)
                if i == 5 and o.real:
                    copy_wrow(o)
                if i == 6 and n.real:
                    low(n, 2)
                    low(n, 3)
                if m.real:
                    for k in range(stats_by[i], stats_by[i + 1]):
                        stats(m, k)
                if n.real:
                    taps1(n, taps1_by[i], taps1_by[i + 1])

        units(dve, step)

    @block.tensor
    def _(pe):
        def taps0(v):
            need(pe, mixed, v.u + 1)
            need(pe, wrow_copied, v.u)
            nc.tensor.matmul(pw[:, 0:B * K0 * K0], t["classes"][:], wmix[v.slot][:], start=True, stop=True).then_inc(taps0_ready, 1)

        def conv0(v, q):
            need(pe, centred, XCHUNKS * v.u + q // 2 + 1)
            need(pe, band0_built, QUADS * v.u + q + 1)
            need(pe, evac0_done, QUADS * v.u + q - 1)
            for b in range(QB):
                image = xt[QB * q // XB][:, (QB * q + b) % XB, :]
                for k, dx in enumerate((1, 0, 2)):
                    a, e = max(0, 1 - dx), W - max(0, dx - 1)
                    ins = nc.tensor.matmul(p0[q % 2][:, b, a:e], band0[q % 2][:, b * K0 + dx, 0:H],
                                           image[:, a + dx - 1:e + dx - 1], start=k == 0, stop=k == 2)
            ins.then_inc(conv0_quad, 1)

        def turn(v, f):
            need(pe, norm_done, NCHUNKS * v.u + f // 2 + 1)
            need(pe, lo_done, FILLS * v.u + f - 1)
            for i in range(FILL):
                tile = norm[f // 2 % 2][:, i, TR * (f % 2):TR * (f % 2 + 1), :].rearrange("p r s -> p (r s)")
                ins = nc.tensor.transpose(pt[f % 2][:, i, :], tile, t["ident"][:])
            ins.then_inc(turned, 1)

        def conv1(v, i):
            need(pe, evac1_done, BANKS * v.u + i - 1)
            w, h = divmod(i, HALVES)
            fills = FILLS * v.u + min(HALVES * (w + 2), FILLS)
            need(pe, hi_done, fills)
            need(pe, lo_done, fills)
            need(pe, taps_chain, 9 * (v.u + 1))
            out = p1[i % 2]
            sources = ((h, 0, 0, TR, REACH), (1 - h, h - 1, 0, REACH, OR - REACH), (1 - h, h, TR - REACH, TR, 0))
            left = BC * w
            whole = range(left // TCOL, (left + BC) // TCOL)
            tiles = [k for k in (*whole, whole[0] - 1, whole[-1] + 1) if 0 <= k < TILES]
            work = []
            for k in tiles:
                a = max(left, TCOL * k - REACH)
                e = min(left + BC, TCOL * k + TCOL + REACH)
                s = a - (TCOL * k - REACH)
                for half, shift, r0, r1, tap in sources:
                    data = slice(B + B * shift, B + B * shift + H)
                    dst = out[:, a - left:e - left, r0:r1]
                    hi, lo = (z[:, half * TILES + k, data] for z in (tile_hi, tile_lo))
                    th, tl = (z[v.slot][:, s:s + e - a, tap:tap + r1 - r0] for z in (taps_hi, taps_lo))
                    work += [(dst, hi, th), (dst, hi, tl), (dst, lo, th)]
            for n, (dst, data, taps) in enumerate(work):
                ins = nc.tensor.matmul(dst, data, taps, start=n == 0, stop=n == len(work) - 1, skip_group_check=True)
            ins.then_inc(conv1_bank, 1)

        def mean(v):
            need(pe, mean_local, v.group + 1)
            nc.tensor.matmul(pst[:, 0:1], t["average"][:], col["msum"][:], start=True, stop=True).then_inc(mean_ready, 1)

        def var(v):
            need(pe, var_local, v.group + 1)
            nc.tensor.matmul(pst[:, 1:2], t["average"][:], col["vsum"][:], start=True, stop=True).then_inc(var_ready, 1)

        pe.wait_ge(pads_zero, 1)

        def step(turn_, j):
            a, n, w, o = Unit(turn_, j), Unit(turn_, j + 1), Unit(turn_, j + 5), Unit(turn_, j + 6)
            scaling = j % GC == GC - 1 and n.real
            if a.real:
                turn(a, 4)
                turn(a, 5)
            for i in range(BANKS):
                if a.real:
                    conv1(a, i)
                if i == 0 and scaling:
                    mean(n)
                if i == 1 and scaling:
                    var(n)
                if w.real:
                    conv0(w, i)
                if i == 0 and a.real:
                    turn(a, 6)
                    turn(a, 7)
                if i == 4 and o.real:
                    taps0(o)
                if i in (4, 6) and n.real:
                    turn(n, i - 4)
                    turn(n, i - 3)

        units(pe, step)


def build(nc, d):
    with ExitStack() as ctx:
        def sem(name):
            return ctx.enter_context(nc.semaphore(name))

        def sb(name, shape, dt=F32):
            return ctx.enter_context(nc.sbuf_tensor(name, shape, dt))

        d["xs"] = d["x"].rearrange("b c h w -> b c (h w)")
        d["x_rows"] = d["x"].rearrange("b c h w -> c h b w")
        d["out_strips"] = d["out"].rearrange("b c (q r) w -> c q b (r w)", q=STRIPS)
        t = {
            "negmean": sb("negmean", [H, G * B]),
            "hidden": sb("hidden", [C, G, B]),
            "w2rot": sb("w2rot", [C, C * K0 * K0]),
            "mask0": sb("mask0", [H, W0]),
            "mask1": sb("mask1", [H, OC * OR]),
            "classes": sb("classes", [C, H]),
            "average": sb("average", [H, H]),
            "ident": sb("ident", [H, H]),
            "biasb": sb("biasb", [H, C]),
            "dm": sb("dm", [H, C * 4]),
            "y0": sb("y0", [H, OR]),
            "y1": sb("y1", [H, OC]),
        }
        with ExitStack() as inner:
            statistics_block(nc, inner, t, d, sem)
        with ExitStack() as inner:
            main_block(nc, inner, t, d, sem)


def constants():
    import numpy as np

    p = np.arange(H)
    c = np.arange(C)
    k = c % 32
    out = {
        "group_sum": (c[:, None] // GC == c[None, :] // GC).astype(np.float32),
        "first_of_group": (c[:, None] == GC * np.arange(G)[None, :]).astype(np.float32),
        "classes": (c[:, None] // 32 == p[None, :] % K0).astype(np.float32),
    }
    h = np.arange(W0)
    out["mask0"] = ((abs(h[None, :] - p[:, None]) <= K0 // 2) & (h[None, :] < H)).astype(np.float32)
    out["average"] = ((p[:, None] % B == p[None, :] % B) / (STRIPS * 2 * GC * SUBS)).astype(np.float32)
    out["ident"] = np.eye(H, dtype=np.float32)
    y0 = p[:, None] // TCOL - np.arange(OR)[None, :] + REACH
    y1 = p[:, None] % TCOL - np.arange(OC)[None, :] + REACH
    out["y0"], out["y1"] = y0.astype(np.float32), y1.astype(np.float32)
    inside = (abs(y1)[:, :, None] <= REACH) & (abs(y0)[:, None, :] <= REACH)
    out["mask1"] = inside.reshape(H, OC * OR).astype(np.float32)
    out["ones_k"] = np.stack([k < RED, k == RED, k == RED + 1], 1).astype(np.float32)
    return out


def kernel(x, L0_conv_w1, L0_conv_gamma, L0_conv_beta, L0_conv_running_mean, L0_conv_running_var,
           L0_conv_w2, L0_conv_b2, L0_conv_bias, L1_conv_diff_metric):
    import numpy as np
    import concourse.bacc as bacc
    from concourse.bass_utils import run_bass_kernel_spmd as run

    f = np.float32
    con = constants()
    w1rep = np.zeros((C, K0, 32), f)
    w1rep[:, :, 0:RED] = np.asarray(L0_conv_w1).T[:, None, :]
    vec = np.zeros((K0, 32, 7), f)
    vec[:, :, 3] = 1.0
    for n, v in enumerate((L0_conv_gamma, L0_conv_beta, L0_conv_running_mean, L0_conv_running_var)):
        vec[:, 0:RED, n] = np.asarray(v)[None, :]
    vec[:, :, 4:7] = con.pop("ones_k").reshape(K0, 32, 3)
    w2 = np.asarray(L0_conv_w2).reshape(C, K0, K0, RED)
    b2 = np.asarray(L0_conv_b2).reshape(C, K0, K0)
    w2rot = np.zeros((K0, 32, C, K0, K0), f)
    for r in range(K0):
        for j in range(K0):
            dy = (r - j + 1) % K0
            w2rot[r, 0:RED, :, :, j] = w2[:, dy, :, :].transpose(2, 0, 1)
            w2rot[r, RED, :, :, j] = b2[:, dy, :]
            if dy == 1:
                w2rot[r, RED + 1, :, 1, j] = 1.0
    arrays = {
        "x": np.ascontiguousarray(x),
        "w1rep": w1rep.reshape(C, C),
        "bnvec": vec.reshape(C, 7),
        "w2rot": w2rot.reshape(C, C * K0 * K0),
        "biasb": np.broadcast_to(np.asarray(L0_conv_bias), (H, C)).copy(),
        "dm": np.broadcast_to(np.asarray(L1_conv_diff_metric).reshape(C, 4), (H, C, 4)).reshape(H, 4 * C).copy(),
        **con,
    }
    nc = bacc.Bacc("TRN2", target_bir_lowering=False, num_devices=1)
    d = {n: nc.dram_tensor(f"in_{n}_dram", a.shape, mybir.dt.from_np(a.dtype), kind="ExternalInput").ap()
         for n, a in arrays.items()}
    d["out"] = nc.dram_tensor("out_0_dram", (B, C, H, W), F32, kind="ExternalOutput").ap()
    build(nc, d)
    r = run(nc, [{f"in_{n}_dram": a for n, a in arrays.items()}], core_ids=[0])
    return r.results[0]["out_0_dram"]
```

```python
from contextlib import ExitStack
import math

import concourse.bass as bass
from concourse import mybir

F32 = mybir.dt.float32
F16 = mybir.dt.float16
ALU = mybir.AluOpType
ACT = mybir.ActivationFunctionType
AX = mybir.AxisListType

B, C, H, W = 32, 96, 128, 128
G = 32
GC = C // G
IMG = H * W
RED = C // 4
EPS = 1e-5

QB = 4
QUADS = B // QB
XB = 8
XCHUNKS = B // XB
BANK = 512

K0 = 3
P0 = -(-H // K0)
W0 = P0 * K0

K1 = 9
REACH = K1 // 2
STRIPS = 4
SR = H // STRIPS
TR, TCOL = 16, 8
HALVES = SR // TR
TILES = W // TCOL
OR, OC = TR + K1 - 1, TCOL + K1 - 1
BC = BANK // TR
BANKS = HALVES * W // BC
FILL = 4
FILLS = HALVES * TILES // FILL
EDGE = REACH * TCOL
PARTS = 3
ACT_EDGES = (("bottom", 0), ("bottom", 1), ("top", 0))
DVE_EDGES = (("bottom", 2), ("top", 1), ("top", 2))
S_MAX = 2.0 ** 60
TAPS_STEPS = 9 + 2 * PARTS
SUBS = SR * W // BANK

LOOP = 6
TURNS = C // LOOP
LEAD = 6

SX = 2.0 ** 8
SW = 2.0 ** 16

ALPHA = 0.65
C1 = 1.0 / math.gamma(1.0 + 1.0 / ALPHA)
C2 = math.sqrt(2.0 * C1)
VAL = 3.0 * (-2.0 + (1.0 + 2.0 * ALPHA) * C2) / ((1.0 + 2.0 * ALPHA) * (-2.0 * C1 + 3.0 * C2))
GAUSS = VAL / (4.0 * math.pi * C1)
POISSON = (1.0 - VAL) * math.gamma(1.5) / math.pi ** 1.5 * C2

CHUNKS = 4
CHUNK = IMG // CHUNKS
BN = 512
STATS = CHUNK // BN


def statistics_block(nc, ctx, t, d, sem):
    def sb(name, shape, dt=F32):
        return ctx.enter_context(nc.sbuf_tensor(name, shape, dt))

    piece = [sb(f"piece{i}", [C, CHUNK]) for i in range(CHUNKS)]
    bn = sb("bn", [C, B, CHUNKS * STATS, 6])
    mv = sb("mv", [C, B, 2])
    small = {n: sb(n, [C, B]) for n in ("gmean", "dev", "var", "vare", "sd", "rs", "t1", "t2", "pooled", "hlin", "hsig", "hm")}
    col = {n: sb(n, [C, 1]) for n in ("rve", "rsd", "rr", "c1", "c2", "bnscale")}
    group_sum = sb("group_sum", [C, C])
    w1rep = sb("w1rep", [C, C])
    bnvec = sb("bnvec", [C, 7])
    first_of_group = sb("first_of_group", [C, G])
    wide = sb("wide", [C, G, B])
    ones = sb("ones", [C, H])

    ps = ctx.enter_context(nc.psum_tensor("ps_small", [H, 512], F32))
    pwide = ctx.enter_context(nc.psum_tensor("ps_wide", [H, 2, 512], F32))

    piece_loaded = [sem(f"piece_loaded{i}") for i in range(CHUNKS)]
    piece_read = sem("piece_read")
    consts_loaded = sem("consts_loaded")
    chain = sem("vector_chain")
    psum_ready = sem("psum_ready")
    to_psum = sem("to_psum")
    ones_set = sem("ones_set")
    to_act = sem("to_act")
    act_done = sem("act_done")

    block = ctx.enter_context(nc.Block())

    @block.sync
    def _(sp):
        for dst, src in ((group_sum, d["group_sum"]), (w1rep, d["w1rep"]), (bnvec, d["bnvec"]),
                         (first_of_group, d["first_of_group"]),
                         *((t[n], d[n]) for n in ("biasb", "dm", "y0", "y1", "mask0", "mask1", "classes",
                                                  "w2rot", "average", "ident"))):
            sp.dma_start(dst[:], src).then_inc(consts_loaded, 16)
        for i in range(CHUNKS):
            sp.dma_start(piece[i][:], d["xs"][0, :, i * CHUNK:(i + 1) * CHUNK]).then_inc(piece_loaded[i], 16)
        with sp.Fori(1, B) as b:
            for i in range(CHUNKS):
                sp.wait_ge(piece_read, CHUNKS * (b - 1) + i + 1)
                sp.dma_start(piece[i][:], d["xs"][bass.ds(b, 1), :, i * CHUNK:(i + 1) * CHUNK]
                             .rearrange("a c n -> (a c) n")).then_inc(piece_loaded[i], 16)

    @block.vector
    def _(dve):
        count = [0]

        def link(ins):
            count[0] += 1
            ins.then_inc(chain, 1)
            dve.wait_ge(chain, count[0])

        with dve.Fori(0, B) as b:
            for i in range(CHUNKS):
                dve.wait_ge(piece_loaded[i], 16 * b + 16)
                for j in range(STATS):
                    ins = dve.bn_stats(bn[:, bass.ds(b, 1), i * STATS + j, :].rearrange("c a s -> c (a s)"),
                                       piece[i][:, j * BN:(j + 1) * BN])
                ins.then_inc(piece_read, 1)
        dve.wait_ge(piece_read, B * CHUNKS)
        for b in range(B):
            ins = dve.bn_aggr(mv[:, b, :], bn[:, b, :, :].rearrange("c n s -> c (n s)"))
        link(ins)
        s = small
        dve.tensor_copy(s["t1"][:], mv[:, :, 0]).then_inc(to_psum, 1)
        dve.wait_ge(psum_ready, 1)
        link(dve.tensor_scalar(s["gmean"][:], ps[0:C, 0:B], 1.0 / GC, None, ALU.mult))
        link(dve.tensor_tensor(s["dev"][:], mv[:, :, 0], s["gmean"][:], ALU.subtract))
        link(dve.tensor_tensor(s["t2"][:], s["dev"][:], s["dev"][:], ALU.mult))
        dve.tensor_tensor(s["var"][:], s["t2"][:], mv[:, :, 1], ALU.add).then_inc(to_psum, 1)
        dve.wait_ge(psum_ready, 2)
        dve.tensor_scalar(s["vare"][:], ps[0:C, B:2 * B], 1.0 / GC, EPS, ALU.mult, ALU.add).then_inc(to_act, 1)
        dve.wait_ge(act_done, 1)
        link(dve.reciprocal(s["rs"][:], s["sd"][:]))
        link(dve.tensor_tensor(s["t1"][:], s["rs"][:], s["rs"][:], ALU.mult))
        link(dve.tensor_tensor(s["t2"][:], s["t1"][:], s["vare"][:], ALU.mult))
        link(dve.tensor_scalar(s["t1"][:], s["t2"][:], -0.5, 1.5, ALU.mult, ALU.add))
        link(dve.tensor_tensor(s["hm"][:], s["rs"][:], s["t1"][:], ALU.mult))
        link(dve.tensor_copy(s["rs"][:], s["hm"][:]))
        dve.tensor_tensor(s["pooled"][:], s["dev"][:], s["rs"][:], ALU.mult).then_inc(to_psum, 1)
        dve.wait_ge(consts_loaded, 16 * 14)
        dve.tensor_scalar(col["rve"][:], bnvec[:, 3:4], EPS, None, ALU.add).then_inc(to_act, 1)
        dve.wait_ge(act_done, 2)
        link(dve.reciprocal(col["rr"][:], col["rsd"][:]))
        link(dve.tensor_tensor(col["c1"][:], col["rr"][:], col["rr"][:], ALU.mult))
        link(dve.tensor_tensor(col["c2"][:], col["c1"][:], col["rve"][:], ALU.mult))
        link(dve.tensor_scalar(col["c1"][:], col["c2"][:], -0.5, 1.5, ALU.mult, ALU.add))
        link(dve.tensor_tensor(col["c2"][:], col["rr"][:], col["c1"][:], ALU.mult))
        link(dve.tensor_tensor(col["bnscale"][:], col["c2"][:], bnvec[:, 0:1], ALU.mult))
        dve.wait_ge(psum_ready, 3)
        dve.tensor_scalar(s["hlin"][:], ps[0:C, 2 * B:3 * B], bnvec[:, 2:3], col["bnscale"][:, 0:1],
                          ALU.subtract, ALU.mult).then_inc(to_act, 1)
        dve.wait_ge(act_done, 3)
        link(dve.tensor_scalar(s["hm"][:], s["hsig"][:], bnvec[:, 4:5], bnvec[:, 5:6], ALU.mult, ALU.add))
        fog = first_of_group[:].unsqueeze(2).broadcast_to([C, G, B])
        dve.tensor_tensor(wide[:], fog, s["gmean"][:].unsqueeze(1).broadcast_to([C, G, B]), ALU.mult).then_inc(to_psum, 1)
        dve.wait_ge(psum_ready, 4)
        pw = pwide[:].rearrange("p a n -> p (a n)")
        link(dve.tensor_scalar(t["negmean"][:], pw, -1.0, None, ALU.mult))
        dve.tensor_tensor(wide[:], fog, s["rs"][:].unsqueeze(1).broadcast_to([C, G, B]), ALU.mult).then_inc(to_psum, 1)
        dve.wait_ge(psum_ready, 5)
        link(dve.tensor_tensor(t["hidden"][:], pw[0:C, :].rearrange("p (g b) -> p g b", b=B),
                               s["hm"][:].unsqueeze(1).broadcast_to([C, G, B]), ALU.mult))
        hid = t["hidden"][:].rearrange("p g b -> p (g b)")
        link(dve.tensor_scalar(hid, hid, bnvec[:, 6:7], None, ALU.add))

    @block.scalar
    def _(act):
        act.wait_ge(to_act, 1)
        nc.scalar.activation(small["sd"][:], small["vare"][:], ACT.Sqrt).then_inc(act_done, 1)
        act.wait_ge(to_act, 2)
        nc.scalar.activation(col["rsd"][:], col["rve"][:], ACT.Sqrt).then_inc(act_done, 1)
        act.wait_ge(to_act, 3)
        nc.scalar.activation(small["hsig"][:], small["hlin"][:], ACT.Sigmoid, bias=bnvec[:, 1:2]).then_inc(act_done, 1)

    @block.gpsimd
    def _(pool):
        nc.gpsimd.memset(ones[:], 1.0).then_inc(ones_set, 1)

    @block.tensor
    def _(pe):
        pe.wait_ge(consts_loaded, 16 * 14)
        pe.wait_ge(ones_set, 1)
        steps = ((group_sum, small["t1"], 0), (group_sum, small["var"], B), (w1rep, small["pooled"], 2 * B))
        for n, (lhs, rhs, at) in enumerate(steps):
            pe.wait_ge(to_psum, n + 1)
            nc.tensor.matmul(ps[0:C, at:at + B], lhs[:], rhs[:], start=True, stop=True).then_inc(psum_ready, 1)
        for n in range(2):
            pe.wait_ge(to_psum, 4 + n)
            for a in range(2):
                ins = nc.tensor.matmul(pwide[:, a, :], ones[:], wide[:].rearrange("c g b -> c (g b)")[:, a * 512:(a + 1) * 512],
                                       start=True, stop=True)
            ins.then_inc(psum_ready, 1)


def main_block(nc, ctx, t, d, sem):
    def sb(name, shape, dt=F32):
        return ctx.enter_context(nc.sbuf_tensor(name, shape, dt))

    xt = [sb(f"xt{k}", [H, XB, W]) for k in range(XCHUNKS)]
    band0 = [sb(f"band0_{i}", [H, QB * K0, W0]) for i in range(2)]
    wmix = sb("wmix", [C, B * K0 * K0])
    wrow = [sb(f"wrow{i}", [H, B * K0 * K0]) for i in range(2)]
    x1row = sb("x1row", [H, B, W])
    strip = [sb(f"strip{j}", [H, SR, W]) for j in range(LOOP)]
    norm = [sb(f"norm{i}", [H, FILL, TR, TCOL]) for i in range(2)]
    tile_hi = sb("tile_hi", [H, HALVES * TILES, H], F16)
    tile_lo = sb("tile_lo", [H, HALVES * TILES, H], F16)
    halo = {e: sb(f"halo_{e}", [PARTS * EDGE, HALVES * TILES, H], F16) for e in ("bottom", "top")}
    taps_halo = [{e: sb(f"taps_{e}{i}", [PARTS * EDGE, OC, REACH], F16) for e in ("bottom", "top")} for i in range(2)]
    taps_hi = [sb(f"taps_hi{i}", [H, OC, OR], F16) for i in range(2)]
    taps_lo = [sb(f"taps_lo{i}", [H, OC, OR], F16) for i in range(2)]
    zr = [sb(f"zr{i}", [H, OR]) for i in range(2)]
    zc = [sb(f"zc{i}", [H, OC]) for i in range(2)]
    za, zb, zd, ze = (sb(n, [H, OC * OR]) for n in ("za", "zb", "zd", "ze"))
    bnp = sb("bnp", [H, GC * SUBS, 6])
    n_sub = GC * SUBS
    dvp = sb("dvp", [H, n_sub, 2])
    sqp = sb("sqp", [H, n_sub, 2])
    vap = sb("vap", [H, n_sub, 2])
    col = {n: sb(n + "1", [H, 1]) for n in ("msum", "vsum", "gm", "vare", "sd", "rs", "s1", "s2", "s3")}
    scale = [sb(f"scale{i}", [H, 1]) for i in range(2)]
    offset = [sb(f"offset{i}", [H, 1]) for i in range(2)]

    def psum(name, shape):
        return ctx.enter_context(nc.psum_tensor(name, shape, F32))

    p0 = [psum(f"p0_{i}", [H, QB, W]) for i in range(2)]
    pt = [psum(f"pt{i}", [H, FILL, H]) for i in range(2)]
    p1 = [psum(f"p1_{i}", [H, BC, TR]) for i in range(2)]
    pw = psum("pw", [H, BANK])
    pst = psum("pst", [H, BANK])

    x_loaded = [sem(f"x_loaded{k}") for k in range(XCHUNKS)]
    centred = sem("centred")
    mixed = sem("mixed")
    taps0_ready = sem("taps0_ready")
    wrow_copied = sem("wrow_copied")
    band0_built = sem("band0_built")
    conv0_quad = sem("conv0_quad")
    evac0_done = sem("evac0_done")
    stripped = sem("stripped")
    bn_done = sem("bn_done")
    mean_local = sem("mean_local")
    mean_ready = sem("mean_ready")
    mean_chain = sem("mean_chain")
    var_sum = sem("var_sum")
    var_local = sem("var_local")
    var_ready = sem("var_ready")
    vare_ready = sem("vare_ready")
    sd_ready = sem("sd_ready")
    scale_chain = sem("scale_chain")
    scales_ready = sem("scales_ready")
    norm_done = sem("norm_done")
    turned = sem("turned")
    hi_done = sem("hi_done")
    lo_done = sem("lo_done")
    halo_act = sem("halo_act")
    halo_dve = sem("halo_dve")
    pads_zero = sem("pads_zero")
    r2_chain = sem("r2_chain")
    r2_ready = sem("r2_ready")
    s_ready = sem("s_ready")
    powers_ready = sem("powers_ready")
    taps_chain = sem("taps_chain")
    conv1_bank = sem("conv1_bank")
    evac1_done = sem("evac1_done")
    stored = [sem(f"stored{j}") for j in range(LOOP)]

    block = ctx.enter_context(nc.Block())

    def tiles_of(f):
        first = f % HALVES * TILES + f // HALVES * FILL
        return slice(first, first + FILL)

    EDGE_PIXELS = {"bottom": slice(H - EDGE, H), "top": slice(0, EDGE)}
    EDGE_ROWS = {"bottom": slice(OR - REACH, OR), "top": slice(0, REACH)}

    def halo_copy(f, edge, part):
        half, other = f % HALVES, 1 - f % HALVES
        src = (tile_hi, tile_hi, tile_lo)[part][EDGE_PIXELS[edge], tiles_of(f), :]
        first = other * TILES + f // HALVES * FILL
        dst = halo[edge][EDGE * part:EDGE * (part + 1), first:first + FILL, :]
        if edge == "bottom" and half == HALVES - 1:
            return dst[:, :, B:H], src[:, :, 0:H - B]
        if edge == "top" and half == 0:
            return dst[:, :, 0:H - B], src[:, :, B:H]
        return dst, src

    def banks_over(f):
        return HALVES * min(f // HALVES + 2, W // BC)

    def known(v):
        return isinstance(v, int)

    class Unit:

        def __init__(self, turn, j):
            self.turn, self.j = turn + j // LOOP, j % LOOP
            self.u = LOOP * self.turn + self.j
            self.slot = self.j % 2
            self.c = self.j % GC
            self.group = LOOP // GC * self.turn + self.j // GC
            self.gslot = self.j // GC % 2
            self.real = not known(self.u) or 0 <= self.u < C

    def need(eng, s, value):
        if not known(value) or value > 0:
            eng.wait_ge(s, value)

    def units(eng, step):
        for j in range(-LEAD, LOOP):
            step(j // LOOP, j % LOOP)
        with eng.Fori(1, TURNS - 1) as turn:
            for j in range(LOOP):
                now = eng.alloc_register(f"turn_of_step{j}")
                eng.reg_mov(now, turn)
                step(eng.snap(now, min_val=1, max_val=TURNS - 2), j)
        for j in range(LOOP):
            step(TURNS - 1, j)

    @block.sync
    def _(sp):
        def load(v):
            for k in range(XCHUNKS):
                need(sp, conv0_quad, QUADS * (v.u - 1) + XB // QB * (k + 1))
                src = d["x_rows"][bass.ds(v.u, 1), :, XB * k:XB * (k + 1), :]
                sp.dma_start(xt[k][:], src.rearrange("a h b w -> h (a b) w")).then_inc(x_loaded[k], 16)

        def store(v):
            need(sp, evac1_done, BANKS * (v.u + 1))
            for q in range(STRIPS):
                dst = d["out_strips"][bass.ds(v.u, 1), q, :, :]
                sp.dma_start(dst.rearrange("a b n -> (a b) n"),
                             strip[v.j][B * q:B * (q + 1), :, :].rearrange("p r w -> p (r w)")).then_inc(stored[v.j], 16)

        def step(turn, j):
            a, o = Unit(turn, j), Unit(turn, j + 6)
            if o.real:
                load(o)
            if a.real:
                store(a)

        units(sp, step)
        for s in stored:
            sp.wait_ge(s, 16 * STRIPS * TURNS)

    @block.scalar
    def _(act):
        def centre(v, k):
            need(act, x_loaded[k], 16 * (v.u + 1))
            for b in range(XB):
                ins = nc.scalar.activation(xt[k][:, b, :], xt[k][:, b, :], ACT.Identity,
                                           bias=t["negmean"][:, bass.ds(B * v.group + XB * k + b, 1)])
            ins.then_inc(centred, 1)

        def root(v):
            need(act, vare_ready, v.group + 1)
            nc.scalar.activation(col["sd"][:], col["vare"][:], ACT.Sqrt).then_inc(sd_ready, 1)

        def normalise(v, k):
            need(act, scales_ready, v.group + 1)
            need(act, turned, FILLS * v.u + k - 1)
            w, h = divmod(k, HALVES)
            nc.scalar.activation(norm[k % 2][:].rearrange("p i r s -> p r i s"),
                                 strip[v.j][:, TR * h:TR * (h + 1), BC * w:BC * (w + 1)]
                                 .rearrange("p r (i s) -> p r i s", s=TCOL),
                                 ACT.Identity, bias=offset[v.gslot][:, 0:1],
                                 scale=scale[v.gslot][:, 0:1]).then_inc(norm_done, 1)

        def high(v, f):
            need(act, turned, FILLS * v.u + f + 1)
            need(act, conv1_bank, BANKS * (v.u - 1) + banks_over(f))
            nc.scalar.activation(tile_hi[:, tiles_of(f), :], pt[f % 2][:], ACT.Copy).then_inc(hi_done, 1)

        def edges(v, f):
            need(act, hi_done, FILLS * v.u + f + 1)
            for edge, part in ACT_EDGES:
                dst, src = halo_copy(f, edge, part)
                ins = nc.scalar.activation(dst, src, ACT.Copy)
            ins.then_inc(halo_act, 1)

        def tap_parts(v):
            need(act, s_ready, v.u + 1)
            need(act, taps_chain, TAPS_STEPS * (v.u - 1) + 9)
            nc.scalar.activation(ze[:], zd[:], ACT.Exp, scale=-1.0 / (4.0 * C1)).then_inc(powers_ready, 1)
            nc.scalar.activation(zb[:], za[:], ACT.Ln).then_inc(powers_ready, 1)
            need(act, powers_ready, 3 * v.u + 2)
            nc.scalar.activation(zb[:], zb[:], ACT.Exp, scale=-0.5).then_inc(powers_ready, 1)

        def pair(v, f, following):
            for k in (f, f + 1):
                high(v, k)
                if following.real:
                    normalise(following, (k + 2) % FILLS)
            for k in (f, f + 1):
                edges(v, k)

        def step(turn, j):
            a, n, w, o = Unit(turn, j), Unit(turn, j + 1), Unit(turn, j + 5), Unit(turn, j + 6)
            if a.real:
                pair(a, 4, a)
            if w.real:
                centre(w, 2)
            if a.real:
                for k in (6, 7):
                    high(a, k)
                for k in (6, 7):
                    edges(a, k)
            if n.real:
                if j % GC == GC - 1:
                    root(n)
                normalise(n, 0)
                normalise(n, 1)
                tap_parts(n)
                pair(n, 0, n)
            if w.real:
                centre(w, 3)
            if o.real:
                centre(o, 0)
            if n.real:
                pair(n, 2, n)
            if o.real:
                centre(o, 1)

        units(act, step)

    @block.gpsimd
    def _(pool):
        def mix(v):
            need(pool, taps0_ready, v.u)
            shape = [C, B, K0 * K0]
            w2c = t["w2rot"][:, bass.ds(K0 * K0 * v.u, K0 * K0)]
            hid = t["hidden"][:].rearrange("k g b -> k (g b)")[:, bass.ds(B * v.group, B)]
            nc.gpsimd.tensor_tensor(wmix[:].rearrange("k (b r) -> k b r", b=B),
                                    w2c.unsqueeze(1).broadcast_to(shape),
                                    hid.unsqueeze(2).broadcast_to(shape), ALU.mult).then_inc(mixed, 1)

        def band(v, q):
            need(pool, wrow_copied, v.u + 1)
            need(pool, conv0_quad, QUADS * v.u + q - 1)
            n = QB * K0
            shape = [H, n, P0, K0]
            taps = wrow[v.slot][:, q * n * K0:(q + 1) * n * K0].rearrange("p (n j) -> p n j", j=K0)
            nc.gpsimd.tensor_tensor(band0[q % 2][:].rearrange("p n (a j) -> p n a j", j=K0),
                                    t["mask0"][:].rearrange("p (a j) -> p a j", j=K0).unsqueeze(1).broadcast_to(shape),
                                    taps.unsqueeze(2).broadcast_to(shape), ALU.mult).then_inc(band0_built, 1)

        def distance(v, part):
            base = 6 * v.u

            def entry(i, n):
                return t["dm"][:, bass.ds(4 * v.u + i, 1)].broadcast_to([H, n])

            def total(i):
                full = [H, OC, OR]
                need(pool, taps_chain, TAPS_STEPS * (v.u - 1) + 6)
                need(pool, r2_chain, base + 2)
                nc.gpsimd.tensor_tensor((za, zd)[i][:].rearrange("p (x y) -> p x y", x=OC),
                                        zr[i][:].unsqueeze(1).broadcast_to(full),
                                        zc[i][:].unsqueeze(2).broadcast_to(full), ALU.add).then_inc(r2_chain, 1)

            if part == 0:
                need(pool, r2_ready, v.u)
                for i in range(2):
                    nc.gpsimd.tensor_tensor(zr[i][:], entry(2 * i, OR), t["y0"][:], ALU.mult)
                    ins = nc.gpsimd.tensor_tensor(zc[i][:], entry(2 * i + 1, OC), t["y1"][:], ALU.mult)
                    ins.then_inc(r2_chain, 1)
                total(0)
            elif part == 1:
                total(1)
                need(pool, r2_chain, base + 3)
                nc.gpsimd.tensor_tensor(za[:], za[:], za[:], ALU.mult).then_inc(r2_chain, 1)
            else:
                need(pool, r2_chain, base + 4)
                nc.gpsimd.tensor_tensor(zd[:], zd[:], zd[:], ALU.mult).then_inc(r2_chain, 1)
                need(pool, r2_chain, base + 6)
                nc.gpsimd.tensor_tensor(zd[:], za[:], zd[:], ALU.add).then_inc(r2_ready, 1)

        def step(turn, j):
            n, w, o = Unit(turn, j + 1), Unit(turn, j + 5), Unit(turn, j + 6)
            for q in range(QUADS):
                if w.real:
                    band(w, q)
                if q < 3 and n.real:
                    distance(n, q)
                if q == 3 and o.real:
                    mix(o)

        units(pool, step)

    @block.vector
    def _(dve):
        def copy_wrow(v):
            need(dve, taps0_ready, v.u + 1)
            need(dve, band0_built, QUADS * (v.u - 1))
            dve.tensor_copy(wrow[v.slot][:], pw[:, 0:B * K0 * K0]).then_inc(wrow_copied, 1)

        def evac0(v, q):
            need(dve, conv0_quad, QUADS * v.u + q + 1)
            if q == 0:
                need(dve, stripped, XCHUNKS * v.u)
            mean = t["negmean"][:, bass.ds(B * v.group + QB * q, QB)].unsqueeze(2).broadcast_to([H, QB, W])
            dve.scalar_tensor_tensor(x1row[:, QB * q:QB * (q + 1), :], p0[q % 2][:], t["biasb"][:, bass.ds(v.u, 1)],
                                     mean, ALU.add, ALU.subtract).then_inc(evac0_done, 1)

        def turn_rows(v, i):
            if i == 0:
                need(dve, evac0_done, QUADS * (v.u + 1))
                need(dve, stored[v.j], 16 * STRIPS * v.turn)
            cols = slice(W // XCHUNKS * i, W // XCHUNKS * (i + 1))
            dve.transpose(strip[v.j][:, :, cols].rearrange("p r w -> p w r"),
                          x1row[:, :, cols].rearrange("p b w -> p w b")).then_inc(stripped, 1)

        def stats(v, i):
            if i == 0:
                need(dve, stripped, XCHUNKS * (v.u + 1))
                if v.c == 0:
                    need(dve, var_local, v.group)
            rows = SR // SUBS
            dve.bn_stats(bnp[:, SUBS * v.c + i, :], strip[v.j][:, rows * i:rows * (i + 1), :]
                         .rearrange("p r w -> p (r w)")).then_inc(bn_done, 1)

        def local_mean(v):
            need(dve, bn_done, SUBS * GC * (v.group + 1))
            need(dve, mean_ready, v.group)
            dve.tensor_reduce(col["msum"][:], bnp[:, :, 1:6:3], AX.XY, ALU.add).then_inc(mean_local, 1)

        def local_var(v):
            base = 3 * v.group
            need(dve, mean_ready, v.group + 1)
            need(dve, scales_ready, v.group)
            dve.tensor_copy(col["gm"][:], pst[:, 0:1]).then_inc(mean_chain, 1)
            need(dve, mean_chain, base + 1)
            dve.tensor_scalar(dvp[:], bnp[:, :, 1:6:3], col["gm"][:, 0:1], None, ALU.subtract).then_inc(mean_chain, 1)
            need(dve, mean_chain, base + 2)
            dve.tensor_tensor(sqp[:], dvp[:], dvp[:], ALU.mult).then_inc(mean_chain, 1)
            need(dve, mean_chain, base + 3)
            dve.scalar_tensor_tensor(vap[:], bnp[:, :, 2:6:3], 2.0 / BANK, sqp[:], ALU.mult, ALU.add).then_inc(var_sum, 1)
            need(dve, var_sum, v.group + 1)
            dve.tensor_reduce(col["vsum"][:], vap[:], AX.XY, ALU.add).then_inc(var_local, 1)

        def scales(v, part):
            base = 5 * v.group
            if part == 0:
                need(dve, var_ready, v.group + 1)
                dve.tensor_scalar(col["vare"][:], pst[:, 1:2], EPS, None, ALU.add).then_inc(vare_ready, 1)
                return
            need(dve, vare_ready, v.group + 1)
            need(dve, sd_ready, v.group + 1)
            dve.reciprocal(col["rs"][:], col["sd"][:]).then_inc(scale_chain, 1)
            need(dve, scale_chain, base + 1)
            dve.tensor_tensor(col["s1"][:], col["rs"][:], col["rs"][:], ALU.mult).then_inc(scale_chain, 1)
            need(dve, scale_chain, base + 2)
            dve.tensor_tensor(col["s2"][:], col["s1"][:], col["vare"][:], ALU.mult).then_inc(scale_chain, 1)
            need(dve, scale_chain, base + 3)
            dve.tensor_scalar(col["s3"][:], col["s2"][:], -0.5 * SX, 1.5 * SX, ALU.mult, ALU.add).then_inc(scale_chain, 1)
            need(dve, scale_chain, base + 4)
            need(dve, norm_done, FILLS * GC * (v.group - 1))
            dve.tensor_tensor(scale[v.gslot][:], col["rs"][:], col["s3"][:], ALU.mult).then_inc(scale_chain, 1)
            need(dve, scale_chain, base + 5)
            dve.scalar_tensor_tensor(offset[v.gslot][:], col["gm"][:], -1.0, scale[v.gslot][:], ALU.mult,
                                     ALU.mult).then_inc(scales_ready, 1)

        def low(v, f):
            need(dve, hi_done, FILLS * v.u + f + 1)
            need(dve, conv1_bank, BANKS * (v.u - 1) + banks_over(f))
            dve.tensor_tensor(tile_lo[:, tiles_of(f), :], pt[f % 2][:], tile_hi[:, tiles_of(f), :],
                              ALU.subtract).then_inc(lo_done, 1)

        def edges(v, f):
            need(dve, lo_done, FILLS * v.u + f + 1)
            for edge, part in DVE_EDGES:
                dst, src = halo_copy(f, edge, part)
                ins = dve.tensor_copy(dst, src)
            ins.then_inc(halo_dve, 1)

        def tap_sum(v):
            need(dve, r2_ready, v.u + 1)
            dve.tensor_scalar(za[:], zd[:], C2 * C2, S_MAX, ALU.add, ALU.min).then_inc(s_ready, 1)

        def taps1(v, first, last):
            base = TAPS_STEPS * v.u
            taps_h = taps_hi[v.slot][:].rearrange("p x y -> p (x y)")
            taps_l = taps_lo[v.slot][:].rearrange("p x y -> p (x y)")
            steps = (
                lambda: dve.tensor_tensor(zd[:], zb[:], zb[:], ALU.mult),
                lambda: dve.scalar_tensor_tensor(zd[:], zd[:], -0.5, za[:], ALU.mult, ALU.mult),
                lambda: dve.scalar_tensor_tensor(zb[:], zd[:], 1.5, zb[:], ALU.add, ALU.mult),
                lambda: dve.tensor_tensor(zd[:], zb[:], zb[:], ALU.mult),
                lambda: dve.tensor_tensor(zd[:], zd[:], zb[:], ALU.mult),
                lambda: dve.scalar_tensor_tensor(ze[:], ze[:], GAUSS / POISSON, zd[:], ALU.mult, ALU.add),
                lambda: dve.scalar_tensor_tensor(zb[:], ze[:], POISSON * SW, t["mask1"][:], ALU.mult, ALU.mult),
                lambda: dve.tensor_copy(taps_h, zb[:]),
                lambda: dve.tensor_tensor(taps_l, zb[:], taps_h, ALU.subtract),
                *(lambda edge=edge, part=part, whole=whole: dve.tensor_copy(
                    taps_halo[v.slot][edge][EDGE * part:EDGE * (part + 1), :, :],
                    whole[v.slot][EDGE_PIXELS[edge], :, EDGE_ROWS[edge]])
                  for edge in ("bottom", "top") for part, whole in enumerate((taps_hi, taps_lo, taps_hi))),
            )
            for k in range(first, last):
                if k == 0:
                    need(dve, powers_ready, 3 * v.u + 3)
                need(dve, taps_chain, base + k)
                steps[k]().then_inc(taps_chain, 1)

        def evac1(v, i):
            need(dve, conv1_bank, BANKS * v.u + i + 1)
            w, h = divmod(i, HALVES)
            part = strip[v.j][:, TR * h:TR * (h + 1), BC * w:BC * (w + 1)]
            dve.scalar_tensor_tensor(part, p1[i % 2][:].rearrange("p c r -> p r c"), 1.0 / (SX * SW), part,
                                     ALU.mult, ALU.add).then_inc(evac1_done, 1)

        dve.memset(halo["bottom"][:, 0:TILES, 0:B], 0.0)
        dve.memset(halo["top"][:, TILES:HALVES * TILES, H - B:H], 0.0).then_inc(pads_zero, 1)

        stats_by = (0, 0, 1, 3, 3, 5, 5, 6, 8)
        taps1_by = (0, 0, 0, 0, 3, 7, 9, TAPS_STEPS, TAPS_STEPS)

        def pair(v, f):
            low(v, f)
            low(v, f + 1)
            edges(v, f)
            edges(v, f + 1)

        def step(turn, j):
            a, n, m = Unit(turn, j), Unit(turn, j + 1), Unit(turn, j + 4)
            w, o = Unit(turn, j + 5), Unit(turn, j + 6)
            scaling = j % GC == GC - 1 and n.real
            if scaling:
                local_mean(n)
            if a.real:
                pair(a, 4)
            if m.real:
                turn_rows(m, 0)
                turn_rows(m, 1)
            if a.real:
                evac1(a, 0)
            if m.real:
                turn_rows(m, 2)
                turn_rows(m, 3)
            if scaling:
                local_var(n)
            for i in range(BANKS):
                if i == 1 and a.real:
                    pair(a, 6)
                if i == 2 and scaling:
                    scales(n, 1)
                if i > 0 and a.real:
                    evac1(a, i)
                if w.real:
                    evac0(w, i)
                if i == 1 and scaling:
                    scales(n, 0)
                if i == 1 and n.real:
                    tap_sum(n)
                if i == 3 and n.real:
                    taps1(n, taps1_by[i], taps1_by[i + 1])
                if i in (3, 5) and n.real:
                    pair(n, i - 3)
                if i == 5 and o.real:
                    copy_wrow(o)
                if i > 3 and n.real:
                    taps1(n, taps1_by[i], taps1_by[i + 1])
                if m.real:
                    for k in range(stats_by[i], stats_by[i + 1]):
                        stats(m, k)

        units(dve, step)

    @block.tensor
    def _(pe):
        def taps0(v):
            need(pe, mixed, v.u + 1)
            need(pe, wrow_copied, v.u)
            nc.tensor.matmul(pw[:, 0:B * K0 * K0], t["classes"][:], wmix[:], start=True, stop=True).then_inc(taps0_ready, 1)

        def conv0(v, q):
            need(pe, centred, XCHUNKS * v.u + q // 2 + 1)
            need(pe, band0_built, QUADS * v.u + q + 1)
            need(pe, evac0_done, QUADS * v.u + q - 1)
            for b in range(QB):
                image = xt[QB * q // XB][:, (QB * q + b) % XB, :]
                for k, dx in enumerate((1, 0, 2)):
                    a, e = max(0, 1 - dx), W - max(0, dx - 1)
                    ins = nc.tensor.matmul(p0[q % 2][:, b, a:e], band0[q % 2][:, b * K0 + dx, 0:H],
                                           image[:, a + dx - 1:e + dx - 1], start=k == 0, stop=k == 2)
            ins.then_inc(conv0_quad, 1)

        def turn(v, f):
            need(pe, norm_done, FILLS * v.u + f + 1)
            need(pe, lo_done, FILLS * v.u + f - 1)
            for i in range(FILL):
                tile = norm[f % 2][:, i, :, :].rearrange("p r s -> p (r s)")
                ins = nc.tensor.transpose(pt[f % 2][:, i, :], tile, t["ident"][:])
            ins.then_inc(turned, 1)

        def conv1(v, i):
            need(pe, evac1_done, BANKS * v.u + i - 1)
            w, h = divmod(i, HALVES)
            fills = FILLS * v.u + min(HALVES * (w + 2), FILLS)
            for done in (hi_done, lo_done, halo_act, halo_dve):
                need(pe, done, fills)
            need(pe, taps_chain, TAPS_STEPS * (v.u + 1))
            out = p1[i % 2]
            left = BC * w
            whole = range(left // TCOL, (left + BC) // TCOL)
            tiles = [k for k in (*whole, whole[0] - 1, whole[-1] + 1) if 0 <= k < TILES]
            work = []
            for k in tiles:
                a = max(left, TCOL * k - REACH)
                e = min(left + BC, TCOL * k + TCOL + REACH)
                dst = out[:, a - left:e - left, :]
                s = slice(a - (TCOL * k - REACH), e - (TCOL * k - REACH))
                hi, lo = (z[:, h * TILES + k, :] for z in (tile_hi, tile_lo))
                th, tl = (z[v.slot][:, s, REACH:REACH + TR] for z in (taps_hi, taps_lo))
                work += [(dst, hi, th), (dst, hi, tl), (dst, lo, th)]
                for edge, rows in (("bottom", slice(0, REACH)), ("top", slice(TR - REACH, TR))):
                    work.append((dst[:, :, rows], halo[edge][:, h * TILES + k, :], taps_halo[v.slot][edge][:, s, :]))
            for n, (dst, data, taps) in enumerate(work):
                ins = nc.tensor.matmul(dst, data, taps, start=n == 0, stop=n == len(work) - 1, skip_group_check=True)
            ins.then_inc(conv1_bank, 1)

        def mean(v):
            need(pe, mean_local, v.group + 1)
            nc.tensor.matmul(pst[:, 0:1], t["average"][:], col["msum"][:], start=True, stop=True).then_inc(mean_ready, 1)

        def var(v):
            need(pe, var_local, v.group + 1)
            nc.tensor.matmul(pst[:, 1:2], t["average"][:], col["vsum"][:], start=True, stop=True).then_inc(var_ready, 1)

        pe.wait_ge(pads_zero, 1)

        def step(turn_, j):
            a, n, w, o = Unit(turn_, j), Unit(turn_, j + 1), Unit(turn_, j + 5), Unit(turn_, j + 6)
            scaling = j % GC == GC - 1 and n.real
            if a.real:
                turn(a, 4)
                turn(a, 5)
            for i in range(BANKS):
                if a.real:
                    conv1(a, i)
                if w.real:
                    conv0(w, i)
                if i == 0 and scaling:
                    mean(n)
                if i == 1 and scaling:
                    var(n)
                if i == 0 and a.real:
                    turn(a, 6)
                    turn(a, 7)
                if i == 4 and o.real:
                    taps0(o)
                if i in (3, 5) and n.real:
                    turn(n, i - 3)
                    turn(n, i - 2)

        units(pe, step)


def build(nc, d):
    with ExitStack() as ctx:
        def sem(name):
            return ctx.enter_context(nc.semaphore(name))

        def sb(name, shape, dt=F32):
            return ctx.enter_context(nc.sbuf_tensor(name, shape, dt))

        d["xs"] = d["x"].rearrange("b c h w -> b c (h w)")
        d["x_rows"] = d["x"].rearrange("b c h w -> c h b w")
        d["out_strips"] = d["out"].rearrange("b c (q r) w -> c q b (r w)", q=STRIPS)
        t = {
            "negmean": sb("negmean", [H, G * B]),
            "hidden": sb("hidden", [C, G, B]),
            "w2rot": sb("w2rot", [C, C * K0 * K0]),
            "mask0": sb("mask0", [H, W0]),
            "mask1": sb("mask1", [H, OC * OR]),
            "classes": sb("classes", [C, H]),
            "average": sb("average", [H, H]),
            "ident": sb("ident", [H, H]),
            "biasb": sb("biasb", [H, C]),
            "dm": sb("dm", [H, C * 4]),
            "y0": sb("y0", [H, OR]),
            "y1": sb("y1", [H, OC]),
        }
        with ExitStack() as inner:
            statistics_block(nc, inner, t, d, sem)
        with ExitStack() as inner:
            main_block(nc, inner, t, d, sem)


def constants():
    import numpy as np

    p = np.arange(H)
    c = np.arange(C)
    k = c % 32
    out = {
        "group_sum": (c[:, None] // GC == c[None, :] // GC).astype(np.float32),
        "first_of_group": (c[:, None] == GC * np.arange(G)[None, :]).astype(np.float32),
        "classes": (c[:, None] // 32 == p[None, :] % K0).astype(np.float32),
    }
    h = np.arange(W0)
    out["mask0"] = ((abs(h[None, :] - p[:, None]) <= K0 // 2) & (h[None, :] < H)).astype(np.float32)
    out["average"] = ((p[:, None] % B == p[None, :] % B) / (STRIPS * 2 * GC * SUBS)).astype(np.float32)
    out["ident"] = np.eye(H, dtype=np.float32)
    y0 = p[:, None] // TCOL - np.arange(OR)[None, :] + REACH
    y1 = p[:, None] % TCOL - np.arange(OC)[None, :] + REACH
    out["y0"], out["y1"] = y0.astype(np.float32), y1.astype(np.float32)
    inside = (abs(y1)[:, :, None] <= REACH) & (abs(y0)[:, None, :] <= REACH)
    out["mask1"] = inside.reshape(H, OC * OR).astype(np.float32)
    out["ones_k"] = np.stack([k < RED, k == RED, k == RED + 1], 1).astype(np.float32)
    return out


def kernel(x, L0_conv_w1, L0_conv_gamma, L0_conv_beta, L0_conv_running_mean, L0_conv_running_var,
           L0_conv_w2, L0_conv_b2, L0_conv_bias, L1_conv_diff_metric):
    import numpy as np
    import concourse.bacc as bacc
    from concourse.bass_utils import run_bass_kernel_spmd as run

    f = np.float32
    con = constants()
    w1rep = np.zeros((C, K0, 32), f)
    w1rep[:, :, 0:RED] = np.asarray(L0_conv_w1).T[:, None, :]
    vec = np.zeros((K0, 32, 7), f)
    vec[:, :, 3] = 1.0
    for n, v in enumerate((L0_conv_gamma, L0_conv_beta, L0_conv_running_mean, L0_conv_running_var)):
        vec[:, 0:RED, n] = np.asarray(v)[None, :]
    vec[:, :, 4:7] = con.pop("ones_k").reshape(K0, 32, 3)
    w2 = np.asarray(L0_conv_w2).reshape(C, K0, K0, RED)
    b2 = np.asarray(L0_conv_b2).reshape(C, K0, K0)
    w2rot = np.zeros((K0, 32, C, K0, K0), f)
    for r in range(K0):
        for j in range(K0):
            dy = (r - j + 1) % K0
            w2rot[r, 0:RED, :, :, j] = w2[:, dy, :, :].transpose(2, 0, 1)
            w2rot[r, RED, :, :, j] = b2[:, dy, :]
            if dy == 1:
                w2rot[r, RED + 1, :, 1, j] = 1.0
    arrays = {
        "x": np.ascontiguousarray(x),
        "w1rep": w1rep.reshape(C, C),
        "bnvec": vec.reshape(C, 7),
        "w2rot": w2rot.reshape(C, C * K0 * K0),
        "biasb": np.broadcast_to(np.asarray(L0_conv_bias), (H, C)).copy(),
        "dm": np.broadcast_to(np.asarray(L1_conv_diff_metric).reshape(C, 4), (H, C, 4)).reshape(H, 4 * C).copy(),
        **con,
    }
    nc = bacc.Bacc("TRN2", target_bir_lowering=False, num_devices=1)
    d = {n: nc.dram_tensor(f"in_{n}_dram", a.shape, mybir.dt.from_np(a.dtype), kind="ExternalInput").ap()
         for n, a in arrays.items()}
    d["out"] = nc.dram_tensor("out_0_dram", (B, C, H, W), F32, kind="ExternalOutput").ap()
    build(nc, d)
    r = run(nc, [{f"in_{n}_dram": a for n, a in arrays.items()}], core_ids=[0])
    return r.results[0]["out_0_dram"]
```
